# Optimizing a Trainium2 kernel written in Bass

```python
import numpy as np
import jax
import jax.numpy as jnp

def _softmax(x, axis=-1):
    return jax.nn.softmax(x, axis=axis)

def _gelu(x):
    return jax.nn.gelu(x, approximate=True)

def _silu(x):
    return jax.nn.silu(x)

def _sigmoid(x):
    return jax.nn.sigmoid(x)

def _layernorm(x, axis=-1, eps=1e-05):
    m = jnp.mean(x, axis=axis, keepdims=True)
    v = jnp.var(x, axis=axis, keepdims=True)
    return (x - m) / jnp.sqrt(v + eps)

def _scatter_add(tgt, idx, src, axis=0):
    return tgt.at[idx].add(src)

def _segment_sum(src, seg, n):
    return jax.ops.segment_sum(src, seg, n)
kernel_name = 'mk_gnn_preln_d2_gnn_r64_95cb95'

def setup_inputs(seed: int=0):
    np.random.seed(seed)
    _w = jnp.asarray

    def _rec_inputs():
        import jax
        import jax.numpy as jnp
        _gk = jax.random.key(seed)
        x = -0.0003713 + 1 * jax.random.normal(jax.random.fold_in(_gk, 1), (50000, 128), jnp.float32)
        src = jax.random.randint(jax.random.fold_in(_gk, 2), (25000,), 0, 50000, jnp.int32)
        dst = jnp.minimum((50000 * jax.random.uniform(jax.random.fold_in(_gk, 3), (25000,)) ** 2.0).astype(jnp.int32), 49999)
        _o = jnp.argsort(dst, stable=True)
        src = src[_o]
        dst = dst[_o]
        edge_attr_64 = 0.000102155 + 1.00015 * jax.random.normal(jax.random.fold_in(_gk, 11), (25000, 64), jnp.float32)
        edge_type_8 = jax.random.randint(jax.random.fold_in(_gk, 13), (25000,), 0, 8, jnp.int32)
        return (x, src, dst, edge_attr_64, edge_type_8)
    x, src, dst, edge_attr_64, edge_type_8 = _rec_inputs()

    def _L0_gnn_setup():
        import jax, jax.numpy as jnp
        import numpy as np
        N_ENT = 100000

        def _rgcn_layer(x, W, SW, b, src, dst, rel):
            xt = jnp.einsum('nd,rde->rne', x, W)
            msg = xt[rel, src]
            agg = jax.ops.segment_sum(msg, dst, num_segments=x.shape[0])
            return jax.nn.relu(agg + x @ SW + b)
        key = jax.random.key(seed)
        ks = jax.random.split(key, 8)
        d, R, E = (128, 8, 9375)
        scale = 1.0 / np.sqrt(d)
        return {'entity_emb': jax.random.normal(ks[0], (N_ENT, d), dtype=jnp.float32), 'w1': jax.random.normal(ks[1], (R, d, d), dtype=jnp.float32) * scale, 'sl1': jax.random.normal(ks[2], (d, d), dtype=jnp.float32) * scale, 'b1': jnp.zeros((d,), dtype=jnp.float32), 'w2': jax.random.normal(ks[3], (R, d, d), dtype=jnp.float32) * scale, 'sl2': jax.random.normal(ks[4], (d, d), dtype=jnp.float32) * scale, 'b2': jnp.zeros((d,), dtype=jnp.float32), 'edge_index': jax.random.randint(ks[5], (2, E), 0, N_ENT, dtype=jnp.int64), 'edge_type': jax.random.randint(ks[6], (E,), 0, R, dtype=jnp.int64)}
    _L0_gnn_all = _L0_gnn_setup()
    _L0_gnn_in = {k: v for k, v in _L0_gnn_all.items() if k in ('w1', 'sl1', 'b1', 'w2', 'sl2', 'b2')}
    del _L0_gnn_all

    def _L1_gnn_setup():
        import jax, jax.numpy as jnp
        import numpy as np
        NODE_DIM, EDGE_DIM, HIDDEN = (128, 64, 128)
        N_NODES, N_EDGES = (50000, 500000)
        EPS = 1e-05

        def layer_norm(h, g, b):
            mu = jnp.mean(h, axis=-1, keepdims=True)
            var = jnp.var(h, axis=-1, keepdims=True)
            return (h - mu) * jax.lax.rsqrt(var + EPS) * g + b
        key = jax.random.key(seed)
        ks = jax.random.split(key, 12)
        s = 0.02
        x = jax.random.normal(ks[0], (N_NODES, NODE_DIM), dtype=jnp.float32)
        edge_index = jax.random.randint(ks[1], (2, N_EDGES), 0, N_NODES, dtype=jnp.int64)
        edge_attr = jax.random.normal(ks[2], (N_EDGES, EDGE_DIM), dtype=jnp.float32)
        eW1 = jax.random.normal(ks[3], (2 * NODE_DIM + EDGE_DIM, HIDDEN), dtype=jnp.float32) * s
        eb1 = jnp.zeros((HIDDEN,), jnp.float32)
        eW2 = jax.random.normal(ks[4], (HIDDEN, HIDDEN), dtype=jnp.float32) * s
        eb2 = jnp.zeros((HIDDEN,), jnp.float32)
        nW1 = jax.random.normal(ks[5], (NODE_DIM + HIDDEN, HIDDEN), dtype=jnp.float32) * s
        nb1 = jnp.zeros((HIDDEN,), jnp.float32)
        nW2 = jax.random.normal(ks[6], (HIDDEN, NODE_DIM), dtype=jnp.float32) * s
        nb2 = jnp.zeros((NODE_DIM,), jnp.float32)
        eg = jnp.ones((HIDDEN,), jnp.float32)
        ebeta = jnp.zeros((HIDDEN,), jnp.float32)
        ng = jnp.ones((NODE_DIM,), jnp.float32)
        nbeta = jnp.zeros((NODE_DIM,), jnp.float32)
        return dict(x=x, edge_index=edge_index, edge_attr=edge_attr, eW1=eW1, eb1=eb1, eW2=eW2, eb2=eb2, nW1=nW1, nb1=nb1, nW2=nW2, nb2=nb2, eg=eg, ebeta=ebeta, ng=ng, nbeta=nbeta)
    _L1_gnn_all = _L1_gnn_setup()
    _L1_gnn_in = {k: v for k, v in _L1_gnn_all.items() if k in ('eW1', 'eb1', 'eW2', 'eb2', 'nW1', 'nb1', 'nW2', 'nb2', 'eg', 'ebeta', 'ng', 'nbeta')}
    del _L1_gnn_all
    return {'x': x, 'src': src, 'dst': dst, 'edge_attr_64': edge_attr_64, 'edge_type_8': edge_type_8, 'L0_gnn_w1': _L0_gnn_in['w1'], 'L0_gnn_sl1': _L0_gnn_in['sl1'], 'L0_gnn_b1': _L0_gnn_in['b1'], 'L0_gnn_w2': _L0_gnn_in['w2'], 'L0_gnn_sl2': _L0_gnn_in['sl2'], 'L0_gnn_b2': _L0_gnn_in['b2'], 'L1_gnn_eW1': _L1_gnn_in['eW1'], 'L1_gnn_eb1': _L1_gnn_in['eb1'], 'L1_gnn_eW2': _L1_gnn_in['eW2'], 'L1_gnn_eb2': _L1_gnn_in['eb2'], 'L1_gnn_nW1': _L1_gnn_in['nW1'], 'L1_gnn_nb1': _L1_gnn_in['nb1'], 'L1_gnn_nW2': _L1_gnn_in['nW2'], 'L1_gnn_nb2': _L1_gnn_in['nb2'], 'L1_gnn_eg': _L1_gnn_in['eg'], 'L1_gnn_ebeta': _L1_gnn_in['ebeta'], 'L1_gnn_ng': _L1_gnn_in['ng'], 'L1_gnn_nbeta': _L1_gnn_in['nbeta']}

def reference(x, src, dst, edge_attr_64, edge_type_8, L0_gnn_w1, L0_gnn_sl1, L0_gnn_b1, L0_gnn_w2, L0_gnn_sl2, L0_gnn_b2, L1_gnn_eW1, L1_gnn_eb1, L1_gnn_eW2, L1_gnn_eb2, L1_gnn_nW1, L1_gnn_nb1, L1_gnn_nW2, L1_gnn_nb2, L1_gnn_eg, L1_gnn_ebeta, L1_gnn_ng, L1_gnn_nbeta):
    import jax
    import jax.numpy as jnp

    def _L0_gnn_ref(entity_emb, w1, sl1, b1, w2, sl2, b2, edge_index, edge_type):
        import jax, jax.numpy as jnp
        import numpy as np
        N_ENT = 100000

        def _rgcn_layer(x, W, SW, b, src, dst, rel):
            xt = jnp.einsum('nd,rde->rne', x, W)
            msg = xt[rel, src]
            agg = jax.ops.segment_sum(msg, dst, num_segments=x.shape[0])
            return jax.nn.relu(agg + x @ SW + b)
        src, dst = (edge_index[0], edge_index[1])
        x = _rgcn_layer(entity_emb, w1, sl1, b1, src, dst, edge_type)
        x = _rgcn_layer(x, w2, sl2, b2, src, dst, edge_type)
        return x

    def _L1_gnn_ref(x, edge_index, edge_attr, eW1, eb1, eW2, eb2, nW1, nb1, nW2, nb2, eg, ebeta, ng, nbeta):
        import jax, jax.numpy as jnp
        import numpy as np
        NODE_DIM, EDGE_DIM, HIDDEN = (128, 64, 128)
        N_NODES, N_EDGES = (50000, 500000)
        EPS = 1e-05

        def layer_norm(h, g, b):
            mu = jnp.mean(h, axis=-1, keepdims=True)
            var = jnp.var(h, axis=-1, keepdims=True)
            return (h - mu) * jax.lax.rsqrt(var + EPS) * g + b
        senders = edge_index[0]
        receivers = edge_index[1]
        edge_input = jnp.concatenate([x[senders], x[receivers], edge_attr], axis=-1)
        h = jax.nn.relu(edge_input @ eW1 + eb1)
        msg = jax.nn.relu(h @ eW2 + eb2)
        msg = layer_norm(msg, eg, ebeta)
        node_agg = jax.ops.segment_sum(msg, receivers, num_segments=x.shape[0])
        node_input = jnp.concatenate([x, node_agg], axis=-1)
        upd = jax.nn.relu(node_input @ nW1 + nb1) @ nW2 + nb2
        return layer_norm(x + upd, ng, nbeta)
    edge_index = jnp.stack([src, dst])
    h = jnp.maximum(_layernorm(x, axis=-1), 0.0)
    x = x + _L0_gnn_ref(h, L0_gnn_w1, L0_gnn_sl1, L0_gnn_b1, L0_gnn_w2, L0_gnn_sl2, L0_gnn_b2, edge_index, edge_type_8)
    h = jnp.maximum(_layernorm(x, axis=-1), 0.0)
    x = x + _L1_gnn_ref(h, edge_index, edge_attr_64, L1_gnn_eW1, L1_gnn_eb1, L1_gnn_eW2, L1_gnn_eb2, L1_gnn_nW1, L1_gnn_nb1, L1_gnn_nW2, L1_gnn_nb2, L1_gnn_eg, L1_gnn_ebeta, L1_gnn_ng, L1_gnn_nbeta)
    return x

_drawn_inputs = setup_inputs


def setup_inputs(seed=0):
    import zlib

    import numpy as np

    out = dict(_drawn_inputs(seed))
    spreads = {'L0_gnn_b1': (0.0, 0.1),
     'L0_gnn_b2': (0.0, 0.1),
     'L1_gnn_eb1': (0.0, 2.0),
     'L1_gnn_eb2': (0.0, 0.8),
     'L1_gnn_nb1': (0.0, 0.681),
     'L1_gnn_nb2': (0.0, 0.1),
     'L1_gnn_eg': (1.0, 0.6),
     'L1_gnn_ebeta': (0.0, 2.0),
     'L1_gnn_ng': (1.0, 0.2),
     'L1_gnn_nbeta': (0.0, 0.1)}
    factors = {'edge_attr_64': 8.0, 'L1_gnn_eW1': 6.704, 'L1_gnn_eW2': 5.299}
    for name, (base, spread) in spreads.items():
        noise = np.random.default_rng([zlib.crc32(name.encode()), seed]).standard_normal(out[name].shape)
        drawn = base * np.exp(spread * noise) if base else spread * noise
        out[name] = jnp.asarray(drawn.astype(out[name].dtype))
    for name, factor in factors.items():
        out[name] = (out[name] * factor).astype(out[name].dtype)
    return out
```

```python
from contextlib import ExitStack

import concourse.bass as bass
from concourse import mybir

F32 = mybir.dt.float32
I32 = mybir.dt.int32
ALU = mybir.AluOpType
ACT = mybir.ActivationFunctionType

P = 128
D = 128
DE = 64
NREL = 8
EPS = 1e-5

NODES = 50000
EDGES = 25000
TILES_E = 196
GT = 4
GROUPS_E = TILES_E // GT
GE = GT * P
DUMP = NODES
PAD_DST = DUMP + 2 * P
ROWS_Z = 50432
NT = 8
GN = NT * P
GROUPS_N = 49
LAST_BASE = NODES - GN

UNROLL = 4
assert GROUPS_E == GROUPS_N == 49
LOOP_END = 11


def sweep(eng, step):
    for u in range(UNROLL):
        step(0, u)
    with eng.Fori(1, LOOP_END) as i:
        for u in range(UNROLL):
            step(i, u)
    for g in range(LOOP_END * UNROLL, GROUPS_N):
        step(g // UNROLL, g % UNROLL)


def ahead(i, u, n):
    v = u + n
    j, w = i + v // UNROLL, v % UNROLL
    if isinstance(j, int) and not 0 <= UNROLL * j + w < GROUPS_N:
        return None
    return j, w


def first(i, u):
    return isinstance(i, int) and i == 0 and u == 0


def wait(eng, sem, value):
    if not (isinstance(value, int) and value <= 0):
        eng.wait_ge(sem, value)


def node_base(i, u):
    g = UNROLL * i + u
    if isinstance(g, int):
        return min(g * GN, LAST_BASE)
    return g * GN


def rows(t, base):
    return t[bass.ds(base, GN), :].rearrange("(p k) d -> p (k d)", p=P)


def setup(nc, sb, sem, a):
    c = {}

    def keep(name, shape, dt=F32):
        c[name] = sb("c_" + name, shape, dt)
        return c[name]

    ident = keep("ident", [P, P])
    earlier = keep("earlier", [P, 2, 2 * P])
    eps = keep("eps", [P, 1])
    zeros = keep("zeros", [P, 4 * D])
    ones_row = keep("ones_row", [1, P])
    src = keep("src", [P, TILES_E], I32)
    dst = keep("dst", [P, TILES_E], I32)
    dstf = keep("dstf", [P, TILES_E])
    dump_less_dst = keep("dump_less_dst", [P, TILES_E])
    keep("scat", [P, TILES_E], I32)
    dump = keep("dump", [P, TILES_E])

    loads = []
    for name in ("w1", "w2"):
        loads.append((keep(name, [P, NREL, D])[:], a[name].rearrange("r d f -> d r f")))
    for name in ("sl1", "sl2", "eW2", "nW2"):
        loads.append((keep(name, [P, D])[:], a[name]))
    loads.append((keep("eW1s", [P, D])[:], a["eW1"][0:D, :]))
    loads.append((keep("eW1d", [P, D])[:], a["eW1"][D:2 * D, :]))
    loads.append((keep("eW1e", [DE, D])[:], a["eW1"][2 * D:2 * D + DE, :]))
    loads.append((keep("nW1x", [P, D])[:], a["nW1"][0:D, :]))
    loads.append((keep("nW1m", [P, D])[:], a["nW1"][D:2 * D, :]))
    for name in ("b1", "b2", "nb1", "eg", "ebeta", "ng", "nbeta"):
        loads.append((keep(name, [P, D])[:], a[name].partition_broadcast(P)))
    loads.append((keep("eb1", [P, 1])[:], a["eb1"].unsqueeze(1)))
    for name in ("eb2", "nb2"):
        t = keep(name, [1, 4, D])
        for k in range(4):
            loads.append((t[0:1, k, :], a[name].unsqueeze(0)))
    loads.append((src[:], a["src"]))
    loads.append((dst[:], a["dst"]))

    loaded, pool_done, zero_done, written = sem("loaded"), sem("pool_done"), sem("zero_done"), sem("written")
    with nc.Block() as block:
        @block.sync
        def _(sp):
            for out, in_ in loads:
                sp.dma_start(out, in_).then_inc(loaded, 16)
            sp.wait_ge(zero_done, 1)
            for z in (a["z1"], a["z2"], a["z3"]):
                rest = ROWS_Z - NODES
                sp.dma_start(z[NODES:NODES + 3 * P, :].rearrange("(p k) d -> p (k d)", p=P),
                             zeros[:, 0:3 * D]).then_inc(written, 16)
                sp.dma_start(z[NODES + 3 * P:ROWS_Z, :], zeros[0:rest - 3 * P, 0:D]).then_inc(written, 16)
            sp.wait_ge(loaded, 16 * len(loads))
            sp.wait_ge(written, 16 * 6)

        @block.vector
        def _(dve):
            nc.vector.memset(zeros[:], 0.0).then_inc(zero_done, 1)
            nc.vector.memset(eps[:], EPS)
            nc.vector.memset(ones_row[:], 1.0)
            dve.wait_ge(loaded, 16 * len(loads))
            nc.vector.tensor_copy(dstf[:], dst[:]).then_inc(zero_done, 1)
            dve.wait_ge(zero_done, 2)
            dve.wait_ge(pool_done, 5)
            nc.vector.tensor_tensor(dump_less_dst[:], dump[:], dstf[:], ALU.subtract)

        @block.gpsimd
        def _(pool):
            nc.gpsimd.memset(ident[:], 0.0).then_inc(pool_done, 1)
            nc.gpsimd.memset(earlier[:], 1.0).then_inc(pool_done, 1)
            pool.wait_ge(pool_done, 2)
            nc.gpsimd.affine_select(out=ident[:], in_=ident[:], compare_op=ALU.not_equal, fill=1.0, base=0,
                                    pattern=[[-1, P]], channel_multiplier=1).then_inc(pool_done, 1)
            nc.gpsimd.affine_select(out=earlier[:], in_=earlier[:], compare_op=ALU.is_gt, fill=0.0, base=0,
                                    pattern=[[P, 2], [-1, 2 * P]], channel_multiplier=1).then_inc(pool_done, 1)
            nc.gpsimd.iota(dump[:], pattern=[[0, TILES_E // 2], [P, 2]], base=DUMP, channel_multiplier=1,
                           allow_small_or_imprecise_dtypes=True).then_inc(pool_done, 1)
            pool.wait_ge(pool_done, 5)
    return c


class Stats:

    def __init__(self, sb, sem, name, n):
        self.n = n
        self.st = sb(name + "_st", [P, n, 6])
        self.small = sb(name + "_small", [P, 4, n])
        self.mean = sb(name + "_mean", [P, 2, n])
        self.var = sb(name + "_var", [P, 2, n])
        self.sd = sb(name + "_sd", [P, n])
        self.rstd = sb(name + "_rstd", [P, 2, n])
        self.step = sem(name + "_step")
        self.var_ready = sem(name + "_var_ready")
        self.sd_ready = sem(name + "_sd_ready")
        self.rstd_ready = sem(name + "_rstd_ready")

    def variances(self, nc, dve, tiles, slot, g):
        st, small = self.st, self.small
        for k in range(self.n):
            ins = nc.vector.bn_stats(st[:, k, :], tiles[k])
        ins.then_inc(self.step, 1)
        dve.wait_ge(self.step, 3 * g + 1)
        nc.vector.tensor_tensor(small[:, 0, :], st[:, :, 1], st[:, :, 4], ALU.subtract)
        nc.vector.tensor_tensor(small[:, 1, :], st[:, :, 1], st[:, :, 4], ALU.add)
        nc.vector.tensor_tensor(small[:, 2, :], st[:, :, 2], st[:, :, 5], ALU.add).then_inc(self.step, 1)
        dve.wait_ge(self.step, 3 * g + 2)
        nc.vector.tensor_scalar(self.mean[:, slot, :], small[:, 1, :], 0.5, None, ALU.mult)
        nc.vector.scalar_tensor_tensor(out=small[:, 3, :], in0=small[:, 0, :], scalar=D / 4.0,
                                       in1=small[:, 0, :], op0=ALU.mult, op1=ALU.mult).then_inc(self.step, 1)
        dve.wait_ge(self.step, 3 * g + 3)
        nc.vector.tensor_tensor(self.var[:, slot, :], small[:, 3, :], small[:, 2, :],
                                ALU.add).then_inc(self.var_ready, 1)

    def deviations(self, nc, act, eps, slot, g):
        act.wait_ge(self.var_ready, g + 1)
        nc.scalar.activation(self.sd[:], self.var[:, slot, :], ACT.Sqrt, bias=eps[:],
                             scale=1.0 / D).then_inc(self.sd_ready, 1)

    def reciprocals(self, nc, dve, slot, g):
        dve.wait_ge(self.sd_ready, g + 1)
        nc.vector.reciprocal(self.rstd[:, slot, :], self.sd[:]).then_inc(self.rstd_ready, 1)
        dve.wait_ge(self.rstd_ready, g + 1)

    def normalise(self, nc, out, in_, k, slot):
        return nc.vector.tensor_scalar(out, in_, self.mean[:, slot, k:k + 1], self.rstd[:, slot, k:k + 1],
                                       ALU.subtract, ALU.mult)


def node_pass(nc, sb, sem, c, ps, name, x, z, w, bias, norm, plus=None, total=None):
    S = lambda n: sem(f"{name}_{n}")
    xin = sb(f"{name}_xin", [P, 4, NT * D])
    if plus is not None:
        pin = sb(f"{name}_pin", [P, 4, NT * D])
        tot = sb(f"{name}_tot", [P, 2, NT * D])
        tot_ready, tot_stored = S("tot_ready"), [S(f"tot_stored{k}") for k in range(2)]
    per_load = 16 if plus is None else 32
    ln = Stats(sb, sem, name, NT) if norm else None
    hT = sb(f"{name}_hT", [P, 2, NT * D])
    zo = sb(f"{name}_zo", [P, 2, NT * D])
    loaded = [S(f"loaded{k}") for k in range(4)]
    stored = [S(f"stored{k}") for k in range(2)]
    normed = S("normed")
    turned, hT_ready, product, z_ready = S("turned"), S("hT_ready"), S("product"), S("z_ready")

    with nc.Block() as block:
        @block.sync
        def _(sp):
            def load(i, u):
                g = UNROLL * i + u
                wait(sp, turned, 2 * (g - 3))
                sp.dma_start(xin[:, u, :], rows(x, node_base(i, u))).then_inc(loaded[u], 16)
                if plus is not None:
                    sp.dma_start(pin[:, u, :], rows(plus, node_base(i, u))).then_inc(loaded[u], 16)

            def store_total(i, u):
                g = UNROLL * i + u
                if isinstance(g, int) and g == GROUPS_N - 1:
                    sp.wait_ge(tot_stored[1 - g % 2], 16 * (g // 2))
                sp.wait_ge(tot_ready, g + 1)
                sp.dma_start(rows(total, node_base(i, u)), tot[:, u % 2, :]).then_inc(tot_stored[u % 2], 16)

            def store(i, u):
                g = UNROLL * i + u
                if isinstance(g, int) and g == GROUPS_N - 1:
                    sp.wait_ge(stored[1 - g % 2], 16 * (g // 2))
                sp.wait_ge(z_ready, 2 * g + 2)
                sp.dma_start(rows(z, node_base(i, u)), zo[:, u % 2, :]).then_inc(stored[u % 2], 16)

            def step(i, u):
                if first(i, u):
                    for k in range(3):
                        load(0, k)
                n = ahead(i, u, 3)
                if n:
                    load(*n)
                if plus is not None:
                    store_total(i, u)
                store(i, u)

            sweep(sp, step)
            sp.wait_ge(stored[0], 16 * (GROUPS_N // 2 + 1))
            sp.wait_ge(stored[1], 16 * (GROUPS_N // 2))
            if plus is not None:
                sp.wait_ge(tot_stored[0], 16 * (GROUPS_N // 2 + 1))
                sp.wait_ge(tot_stored[1], 16 * (GROUPS_N // 2))

        @block.vector
        def _(dve):
            def stats_of(i, u):
                g = UNROLL * i + u
                dve.wait_ge(loaded[u], per_load * (i + 1))
                rows_in = xin[:, u, :]
                if plus is not None:
                    wait(dve, tot_stored[u % 2], 16 * (2 * i + u // 2))
                    rows_in = tot[:, u % 2, :]
                    nc.vector.scalar_tensor_tensor(out=rows_in, in0=pin[:, u, :], scalar=0.0, in1=xin[:, u, :],
                                                   op0=ALU.max, op1=ALU.add).then_inc(tot_ready, 1)
                    dve.wait_ge(tot_ready, g + 1)
                tiles = [rows_in[:, k * D:(k + 1) * D] for k in range(NT)]
                ln.variances(nc, dve, tiles, u % 2, g)

            def normalise(i, u):
                g = UNROLL * i + u
                ln.reciprocals(nc, dve, u % 2, g)
                for k in range(NT):
                    cols = slice(k * D, (k + 1) * D)
                    rows_in = xin[:, u, cols] if plus is None else tot[:, u % 2, cols]
                    ins = ln.normalise(nc, xin[:, u, cols], rows_in, k, u % 2)
                ins.then_inc(normed, 1)

            def finish(i, u):
                g = UNROLL * i + u
                wait(dve, stored[u % 2], 16 * (2 * i + u // 2))
                for h in range(2):
                    dve.wait_ge(product, 2 * g + h + 1)
                    nc.vector.tensor_tensor(
                        zo[:, u % 2, h * 512:(h + 1) * 512].rearrange("p (k d) -> p k d", d=D),
                        ps[:, 4 + 2 * (u % 2) + h, :].rearrange("p (k d) -> p k d", d=D),
                        bias[:].unsqueeze(1).broadcast_to([P, 4, D]), ALU.add).then_inc(z_ready, 1)

            def step(i, u):
                if norm:
                    if first(i, u):
                        stats_of(0, 0)
                        normalise(0, 0)
                    n = ahead(i, u, 1)
                    if n:
                        stats_of(*n)
                        normalise(*n)
                finish(i, u)

            sweep(dve, step)

        @block.scalar
        def _(act):
            def evacuate(i, u):
                g = UNROLL * i + u
                wait(act, product, 2 * g - 2)
                for h in range(2):
                    act.wait_ge(turned, 2 * g + h + 1)
                    nc.scalar.activation(hT[:, u % 2, h * 512:(h + 1) * 512], ps[:, 2 * (u % 2) + h, :],
                                         ACT.Relu).then_inc(hT_ready, 1)

            def step(i, u):
                if norm:
                    if first(i, u):
                        ln.deviations(nc, act, c["eps"], 0, 0)
                evacuate(i, u)
                n = ahead(i, u, 1)
                if norm and n:
                    ln.deviations(nc, act, c["eps"], n[1] % 2, UNROLL * n[0] + n[1])

            sweep(act, step)

        @block.tensor
        def _(pe):
            def turn(i, u):
                g = UNROLL * i + u
                if norm:
                    pe.wait_ge(normed, g + 1)
                else:
                    pe.wait_ge(loaded[u], 16 * (i + 1))
                wait(pe, hT_ready, 2 * (g - 1))
                for k in range(NT):
                    ins = nc.tensor.transpose(ps[:, 2 * (u % 2) + k // 4, (k % 4) * P:(k % 4 + 1) * P],
                                              xin[:, u, k * D:(k + 1) * D], c["ident"][:])
                    if k % 4 == 3:
                        ins.then_inc(turned, 1)

            def multiply(i, u):
                g = UNROLL * i + u
                wait(pe, z_ready, 2 * (g - 1))
                for k in range(NT):
                    if k % 4 == 0:
                        pe.wait_ge(hT_ready, 2 * g + k // 4 + 1)
                    ins = nc.tensor.matmul(ps[:, 4 + 2 * (u % 2) + k // 4, (k % 4) * D:(k % 4 + 1) * D],
                                           hT[:, u % 2, k * P:(k + 1) * P], w[:], start=True, stop=True)
                    if k % 4 == 3:
                        ins.then_inc(product, 1)

            def step(i, u):
                if first(i, u):
                    turn(0, 0)
                multiply(i, u)
                n = ahead(i, u, 1)
                if n:
                    turn(*n)

            sweep(pe, step)


def edge_pass_relational(nc, sb, sem, c, ps, a, name, x, z, w, norm):
    S = lambda n: sem(f"{name}_{n}")
    xg = sb(f"{name}_xg", [P, UNROLL, GE])
    src_ring = sb(f"{name}_src_ring", [P, UNROLL, GT], I32)
    scat_ring = sb(f"{name}_scat_ring", [P, UNROLL, GT], I32)
    type_row = sb(f"{name}_type_row", [P, 2, GE], I32)
    dst_row = sb(f"{name}_dst_row", [P, 2, GE], I32)
    hT = sb(f"{name}_hT", [P, 2, GE])
    masked = sb(f"{name}_masked", [P, 2, NREL, GE])
    msg = sb(f"{name}_msg", [P, 2, GE])
    same = sb(f"{name}_same", [P, 2, GT, 2 * P])
    summed = sb(f"{name}_summed", [P, 2, GE])
    ln = Stats(sb, sem, name, GT) if norm else None
    if norm:
        before = sb(f"{name}_before", [P, 2 * P])
        count = sb(f"{name}_count", [P, GT])
        shift = sb(f"{name}_shift", [P, GT])
        scat_step = S("scat_step")
    gathered = [S(f"gathered{k}") for k in range(UNROLL)]
    rows_in = [S(f"rows_in{k}") for k in range(2)]
    src_ready, scat_ready, added, issuing = S("src_ready"), S("scat_ready"), S("added"), S("issuing")
    normed, turned, hT_ready, mask_ready = S("normed"), S("turned"), S("hT_ready"), S("mask_ready")
    product, msg_ready, same_ready = S("product"), S("msg_ready"), S("same_ready")
    pair_product, summed_ready = S("pair_product"), S("summed_ready")

    with nc.Block() as block:
        @block.sync
        def _(sp):
            def load(i, u):
                g = UNROLL * i + u
                wait(sp, scat_ready, g - 1)
                edges = bass.ds(g * GE, GE)
                sp.dma_start(type_row[:, u % 2, :], a["type"][edges].partition_broadcast(P)).then_inc(rows_in[u % 2], 16)
                sp.dma_start(dst_row[:, u % 2, :], a["dst_line"][edges].partition_broadcast(P)).then_inc(rows_in[u % 2], 16)

            def step(i, u):
                if first(i, u):
                    load(0, 0)
                n = ahead(i, u, 1)
                if n:
                    load(*n)

            sweep(sp, step)

        @block.gpsimd
        def _(pool):
            def gather(i, u, q):
                g = UNROLL * i + u
                if q == 0:
                    pool.wait_ge(src_ready, g + 1)
                    wait(pool, turned, g - 3)
                    pool.sem_inc(issuing, 1)
                for t in (2 * q, 2 * q + 1):
                    pool.indirect_dma_start(
                        xg[:, u, t * D:(t + 1) * D], None, x,
                        bass.IndirectOffsetOnAxis(ap=src_ring[:, u, t:t + 1], axis=0)).then_inc(gathered[u], 16)

            def scatter(i, u, q):
                g = UNROLL * i + u
                if q == 0:
                    pool.wait_ge(summed_ready, g + 1)
                    pool.wait_ge(scat_ready, g + 1)
                wait(pool, added, 32 * (2 * g + q))
                pool.sem_inc(issuing, 1)
                for t in (2 * q, 2 * q + 1):
                    pool.indirect_dma_start(
                        z, bass.IndirectOffsetOnAxis(ap=scat_ring[:, u, t:t + 1], axis=0),
                        summed[:, u % 2, t * D:(t + 1) * D], None, compute_op=ALU.add).then_inc(added, 16)

            def step(i, u):
                if first(i, u):
                    for k in range(3):
                        gather(0, k, 0)
                        gather(0, k, 1)
                n, m = ahead(i, u, 3), ahead(i, u, -1)
                for q in range(2):
                    if n:
                        gather(*n, q)
                    if m:
                        scatter(*m, q)

            sweep(pool, step)
            scatter(GROUPS_E // UNROLL, 0, 0)
            scatter(GROUPS_E // UNROLL, 0, 1)
            pool.wait_ge(added, 64 * GROUPS_E)

        @block.vector
        def _(dve):
            def sources(i, u):
                g = UNROLL * i + u
                wait(dve, gathered[u], 64 * i)
                nc.vector.tensor_scalar(src_ring[:, u, :], c["src"][:, bass.ds(g * GT, GT)], 0.0, None, ALU.add).then_inc(src_ready, 1)

            def variances(i, u):
                dve.wait_ge(gathered[u], 64 * (i + 1))
                ln.variances(nc, dve, [xg[:, u, t * D:(t + 1) * D] for t in range(GT)], u % 2, UNROLL * i + u)

            def normalise(i, u):
                ln.reciprocals(nc, dve, u % 2, UNROLL * i + u)
                for t in range(GT):
                    tile = xg[:, u, t * D:(t + 1) * D]
                    ins = ln.normalise(nc, tile, tile, t, u % 2)
                ins.then_inc(normed, 1)

            def masks(i, u):
                g = UNROLL * i + u
                dve.wait_ge(rows_in[u % 2], 32 * (2 * i + u // 2 + 1))
                dve.wait_ge(hT_ready, g + 1)
                wait(dve, product, g - 1)
                for r in range(NREL):
                    nc.vector.scalar_tensor_tensor(out=masked[:, u % 2, r, :], in0=type_row[:, u % 2, :],
                                                   scalar=float(r), in1=hT[:, u % 2, :],
                                                   op0=ALU.is_equal, op1=ALU.mult).then_inc(mask_ready, 1)

            def equalities(i, u):
                g = UNROLL * i + u
                wait(dve, pair_product, g - 1)
                for t in range(GT):
                    pair = slice(t // 2 * 2 * P, (t // 2 + 1) * 2 * P)
                    ins = nc.vector.tensor_scalar(same[:, u % 2, t, :], dst_row[:, u % 2, pair],
                                                  c["dstf"][:, bass.ds(g * GT + t, 1)], None, ALU.is_equal)
                    if norm:
                        wait(dve, scat_step, 6 * g + t)
                        nc.vector.scalar_tensor_tensor(
                            out=before[:], in0=dst_row[:, u % 2, pair], scalar=c["dstf"][:, bass.ds(g * GT + t, 1)],
                            in1=c["earlier"][:, t % 2, :], op0=ALU.is_equal, op1=ALU.mult,
                            accum_out=count[:, t:t + 1]).then_inc(scat_step, 1)
                ins.then_inc(same_ready, 1)

            def scatter_rows(i, u):
                g = UNROLL * i + u
                here = bass.ds(g * GT, GT)
                if norm:
                    dve.wait_ge(scat_step, 6 * g + 4)
                    nc.vector.scalar_tensor_tensor(out=shift[:], in0=count[:], scalar=1.0,
                                                   in1=c["dump_less_dst"][:, here],
                                                   op0=ALU.min, op1=ALU.mult).then_inc(scat_step, 1)
                    dve.wait_ge(scat_step, 6 * g + 5)
                    nc.vector.tensor_tensor(c["scat"][:, here], shift[:], c["dstf"][:, here],
                                            ALU.add).then_inc(scat_step, 1)
                    dve.wait_ge(scat_step, 6 * g + 6)
                wait(dve, added, 64 * (g - 3))
                nc.vector.tensor_scalar(scat_ring[:, u, :], c["scat"][:, here], 0.0, None, ALU.add).then_inc(scat_ready, 1)

            def step(i, u):
                if first(i, u):
                    for k in range(UNROLL):
                        sources(0, k)
                    if norm:
                        variances(0, 0)
                        normalise(0, 0)
                n = ahead(i, u, 1)
                if n and norm:
                    variances(*n)
                masks(i, u)
                if n and norm:
                    normalise(*n)
                equalities(i, u)
                scatter_rows(i, u)
                n = ahead(i, u, 4)
                if n:
                    sources(*n)

            sweep(dve, step)

        @block.scalar
        def _(act):
            def turned_rows(i, u):
                g = UNROLL * i + u
                act.wait_ge(turned, g + 1)
                wait(act, mask_ready, NREL * (g - 1))
                nc.scalar.activation(hT[:, u % 2, :], ps[:, u % 2, :], ACT.Relu).then_inc(hT_ready, 1)

            def messages(i, u):
                g = UNROLL * i + u
                act.wait_ge(product, g + 1)
                wait(act, pair_product, g - 1)
                nc.scalar.copy(msg[:, u % 2, :], ps[:, 2 + u % 2, :]).then_inc(msg_ready, 1)

            def sums(i, u):
                g = UNROLL * i + u
                act.wait_ge(pair_product, g + 1)
                wait(act, added, 64 * (g - 1))
                nc.scalar.copy(summed[:, u % 2, :], ps[:, 4 + u % 2, :]).then_inc(summed_ready, 1)

            def step(i, u):
                if first(i, u):
                    if norm:
                        ln.deviations(nc, act, c["eps"], 0, 0)
                    turned_rows(0, 0)
                m, n = ahead(i, u, -1), ahead(i, u, 1)
                if m:
                    sums(*m)
                if n and norm:
                    ln.deviations(nc, act, c["eps"], n[1] % 2, UNROLL * n[0] + n[1])
                messages(i, u)
                if n:
                    turned_rows(*n)

            sweep(act, step)
            sums(GROUPS_E // UNROLL, 0)

        @block.tensor
        def _(pe):
            def turn(i, u):
                g = UNROLL * i + u
                if norm:
                    pe.wait_ge(normed, g + 1)
                else:
                    pe.wait_ge(gathered[u], 64 * (i + 1))
                wait(pe, hT_ready, g - 1)
                for t in range(GT):
                    ins = nc.tensor.transpose(ps[:, u % 2, t * P:(t + 1) * P], xg[:, u, t * D:(t + 1) * D],
                                              c["ident"][:])
                ins.then_inc(turned, 1)

            def multiply(i, u):
                g = UNROLL * i + u
                wait(pe, msg_ready, g - 1)
                for r in range(NREL):
                    pe.wait_ge(mask_ready, NREL * g + r + 1)
                    for t in range(GT):
                        ins = nc.tensor.matmul(ps[:, 2 + u % 2, t * D:(t + 1) * D],
                                               masked[:, u % 2, r, t * P:(t + 1) * P], w[:, r, :],
                                               start=(r == 0 and t == 0), stop=(r == NREL - 1),
                                               skip_group_check=True)
                ins.then_inc(product, 1)

            def add_pairs(i, u):
                g = UNROLL * i + u
                pe.wait_ge(msg_ready, g + 1)
                pe.wait_ge(same_ready, g + 1)
                wait(pe, summed_ready, g - 1)
                for t in range(GT):
                    for s in range(2):
                        other = t // 2 * 2 + s
                        ins = nc.tensor.matmul(ps[:, 4 + u % 2, t * D:(t + 1) * D],
                                               same[:, u % 2, other, (t % 2) * P:(t % 2 + 1) * P],
                                               msg[:, u % 2, other * D:(other + 1) * D],
                                               start=(s == 0), stop=(s == 1))
                ins.then_inc(pair_product, 1)

            def step(i, u):
                if first(i, u):
                    turn(0, 0)
                m, n = ahead(i, u, -1), ahead(i, u, 1)
                if m:
                    add_pairs(*m)
                multiply(i, u)
                if n:
                    turn(*n)

            sweep(pe, step)
            add_pairs(GROUPS_E // UNROLL, 0)


def edge_pass_messages(nc, sb, sem, c, ps, a):
    S = lambda n: sem(f"E3_{n}")
    ends = sb("E3_ends", [P, UNROLL, 2 * GE])
    edge = sb("E3_edge", [P, UNROLL, GT * DE])
    src_ring = sb("E3_src_ring", [P, UNROLL, GT], I32)
    dst_ring = sb("E3_dst_ring", [P, UNROLL, GT], I32)
    scat_ring = sb("E3_scat_ring", [P, UNROLL, GT], I32)
    dst_row = sb("E3_dst_row", [P, UNROLL, GE], I32)
    endsT = sb("E3_endsT", [P, 2, GE])
    edgeT = sb("E3_edgeT", [DE, GE])
    hidden = sb("E3_hidden", [P, GE])
    msg = sb("E3_msg", [P, GE])
    scaled = sb("E3_scaled", [P, GE])
    normal = sb("E3_normal", [P, 2, GE])
    same = sb("E3_same", [P, 2, GT, 2 * P])
    summedT = sb("E3_summedT", [P, GE])
    summed = sb("E3_summed", [P, 2, GE])
    lx = Stats(sb, sem, "E3x", 2 * GT)
    lm = Stats(sb, sem, "E3m", GT)
    gathered = [S(f"gathered{k}") for k in range(UNROLL)]
    rows_in = [S(f"rows_in{k}") for k in range(UNROLL)]
    ends_ready, scat_ready, added, issuing = S("ends_ready"), S("scat_ready"), S("added"), S("issuing")
    normed, turned, turned_out, hidden_product = S("normed"), S("turned"), S("turned_out"), S("hidden_product")
    hidden_ready, msg_product, msg_ready = S("hidden_ready"), S("msg_product"), S("msg_ready")
    scaled_step, normal_ready, same_ready = S("scaled_step"), S("normal_ready"), S("same_ready")
    pair_product, summedT_ready, out_product, summed_ready = (
        S("pair_product"), S("summedT_ready"), S("out_product"), S("summed_ready"))

    with nc.Block() as block:
        @block.sync
        def _(sp):
            def load(i, u):
                g = UNROLL * i + u
                wait(sp, turned, g - 3)
                wait(sp, same_ready, g - 3)
                edges = bass.ds(g * GE, GE)
                sp.dma_start(edge[:, u, :].rearrange("p (t f) -> p t f", t=GT),
                             a["edge"][edges, :].rearrange("(t p) f -> p t f", p=P)).then_inc(rows_in[u], 16)
                sp.dma_start(dst_row[:, u, :], a["dst_line"][edges].partition_broadcast(P)).then_inc(rows_in[u], 16)

            def step(i, u):
                if first(i, u):
                    for k in range(3):
                        load(0, k)
                n = ahead(i, u, 3)
                if n:
                    load(*n)

            sweep(sp, step)

        @block.gpsimd
        def _(pool):
            def gather(i, u, q):
                g = UNROLL * i + u
                if q == 0:
                    pool.wait_ge(ends_ready, 2 * g + 2)
                    wait(pool, turned, g - 3)
                    pool.sem_inc(issuing, 1)
                for t in (2 * q, 2 * q + 1):
                    for side, ring in enumerate((src_ring, dst_ring)):
                        at = (side * GT + t) * D
                        pool.indirect_dma_start(
                            ends[:, u, at:at + D], None, a["x2"],
                            bass.IndirectOffsetOnAxis(ap=ring[:, u, t:t + 1], axis=0)).then_inc(gathered[u], 16)

            def scatter(i, u, q):
                g = UNROLL * i + u
                if q == 0:
                    pool.wait_ge(summed_ready, g + 1)
                    pool.wait_ge(scat_ready, g + 1)
                wait(pool, added, 32 * (2 * g + q))
                pool.sem_inc(issuing, 1)
                for t in (2 * q, 2 * q + 1):
                    pool.indirect_dma_start(
                        a["z3"], bass.IndirectOffsetOnAxis(ap=scat_ring[:, u, t:t + 1], axis=0),
                        summed[:, u % 2, t * D:(t + 1) * D], None, compute_op=ALU.add).then_inc(added, 16)

            def step(i, u):
                if first(i, u):
                    for k in range(3):
                        gather(0, k, 0)
                        gather(0, k, 1)
                n, m = ahead(i, u, 3), ahead(i, u, -1)
                for q in range(2):
                    if n:
                        gather(*n, q)
                    if m:
                        scatter(*m, q)

            sweep(pool, step)
            scatter(GROUPS_E // UNROLL, 0, 0)
            scatter(GROUPS_E // UNROLL, 0, 1)
            pool.wait_ge(added, 64 * GROUPS_E)

        @block.vector
        def _(dve):
            def ring_rows(i, u):
                here = bass.ds((UNROLL * i + u) * GT, GT)
                wait(dve, gathered[u], 128 * i)
                nc.vector.tensor_scalar(src_ring[:, u, :], c["src"][:, here], 0.0, None, ALU.add).then_inc(ends_ready, 1)
                nc.vector.tensor_scalar(dst_ring[:, u, :], c["dst"][:, here], float(NODES - 1), None,
                                        ALU.min).then_inc(ends_ready, 1)

            def variances(i, u):
                dve.wait_ge(gathered[u], 128 * (i + 1))
                lx.variances(nc, dve, [ends[:, u, t * D:(t + 1) * D] for t in range(2 * GT)], u % 2, UNROLL * i + u)

            def normalise(i, u):
                lx.reciprocals(nc, dve, u % 2, UNROLL * i + u)
                for t in range(2 * GT):
                    tile = ends[:, u, t * D:(t + 1) * D]
                    ins = lx.normalise(nc, tile, tile, t, u % 2)
                ins.then_inc(normed, 1)

            def equalities(i, u):
                g = UNROLL * i + u
                dve.wait_ge(rows_in[u], 32 * (i + 1))
                wait(dve, pair_product, g - 1)
                for t in range(GT):
                    pair = slice(t // 2 * 2 * P, (t // 2 + 1) * 2 * P)
                    ins = nc.vector.tensor_scalar(same[:, u % 2, t, :], dst_row[:, u, pair],
                                                  c["dstf"][:, bass.ds(g * GT + t, 1)], None, ALU.is_equal)
                ins.then_inc(same_ready, 1)
                wait(dve, added, 64 * (g - 3))
                nc.vector.tensor_scalar(scat_ring[:, u, :], c["scat"][:, bass.ds(g * GT, GT)], 0.0, None, ALU.add).then_inc(scat_ready, 1)

            def message_variances(i, u):
                g = UNROLL * i + u
                dve.wait_ge(msg_ready, g + 1)
                lm.variances(nc, dve, [msg[:, t * D:(t + 1) * D] for t in range(GT)], u % 2, g)

            def message_norm(i, u):
                g = UNROLL * i + u
                lm.reciprocals(nc, dve, u % 2, g)
                for t in range(GT):
                    tile = slice(t * D, (t + 1) * D)
                    ins = lm.normalise(nc, scaled[:, tile], msg[:, tile], t, u % 2)
                ins.then_inc(scaled_step, 1)
                tiles = lambda t: t.rearrange("p (t d) -> p t d", t=GT)
                dve.wait_ge(scaled_step, 2 * g + 1)
                nc.vector.tensor_tensor(tiles(scaled[:]), tiles(scaled[:]),
                                        c["eg"][:].unsqueeze(1).broadcast_to([P, GT, D]),
                                        ALU.mult).then_inc(scaled_step, 1)
                dve.wait_ge(scaled_step, 2 * g + 2)
                wait(dve, pair_product, g - 1)
                nc.vector.tensor_tensor(tiles(normal[:, u % 2, :]), tiles(scaled[:]),
                                        c["ebeta"][:].unsqueeze(1).broadcast_to([P, GT, D]),
                                        ALU.add).then_inc(normal_ready, 1)

            def step(i, u):
                if first(i, u):
                    for k in range(UNROLL):
                        ring_rows(0, k)
                    variances(0, 0)
                    normalise(0, 0)
                n = ahead(i, u, 1)
                if n:
                    variances(*n)
                equalities(i, u)
                if n:
                    normalise(*n)
                message_variances(i, u)
                message_norm(i, u)
                n = ahead(i, u, 4)
                if n:
                    ring_rows(*n)

            sweep(dve, step)

        @block.scalar
        def _(act):
            def turned_rows(i, u):
                g = UNROLL * i + u
                act.wait_ge(turned, g + 1)
                wait(act, hidden_product, g)
                for side in range(2):
                    nc.scalar.activation(endsT[:, side, :], ps[:, side, :], ACT.Relu)
                nc.scalar.copy(edgeT[:], ps[0:DE, 2, :]).then_inc(turned_out, 1)

            def hidden_rows(i, u):
                g = UNROLL * i + u
                act.wait_ge(hidden_product, g + 1)
                wait(act, msg_product, g)
                nc.scalar.activation(hidden[:], ps[:, 3, :], ACT.Relu, bias=c["eb1"][:]).then_inc(hidden_ready, 1)

            def messages(i, u):
                g = UNROLL * i + u
                act.wait_ge(msg_product, g + 1)
                wait(act, scaled_step, 2 * g)
                nc.scalar.activation(msg[:], ps[:, 4, :], ACT.Relu).then_inc(msg_ready, 1)

            def sums_turned(i, u):
                g = UNROLL * i + u
                act.wait_ge(pair_product, g + 1)
                wait(act, out_product, g)
                nc.scalar.copy(summedT[:], ps[:, 5, :]).then_inc(summedT_ready, 1)

            def sums(i, u):
                g = UNROLL * i + u
                act.wait_ge(out_product, g + 1)
                wait(act, added, 64 * (g - 1))
                nc.scalar.copy(summed[:, u % 2, :], ps[:, 6, :]).then_inc(summed_ready, 1)

            def step(i, u):
                if first(i, u):
                    lx.deviations(nc, act, c["eps"], 0, 0)
                    turned_rows(0, 0)
                m, n = ahead(i, u, -1), ahead(i, u, 1)
                hidden_rows(i, u)
                if m:
                    sums_turned(*m)
                if n:
                    lx.deviations(nc, act, c["eps"], n[1] % 2, UNROLL * n[0] + n[1])
                messages(i, u)
                if m:
                    sums(*m)
                lm.deviations(nc, act, c["eps"], u % 2, UNROLL * i + u)
                if n:
                    turned_rows(*n)

            sweep(act, step)
            sums_turned(GROUPS_E // UNROLL, 0)
            sums(GROUPS_E // UNROLL, 0)

        @block.tensor
        def _(pe):
            def turn(i, u):
                g = UNROLL * i + u
                pe.wait_ge(normed, g + 1)
                pe.wait_ge(rows_in[u], 32 * (i + 1))
                wait(pe, turned_out, g)
                for t in range(2 * GT):
                    nc.tensor.transpose(ps[:, t // GT, (t % GT) * P:(t % GT + 1) * P],
                                        ends[:, u, t * D:(t + 1) * D], c["ident"][:])
                for t in range(GT):
                    ins = nc.tensor.transpose(ps[0:DE, 2, t * P:(t + 1) * P], edge[:, u, t * DE:(t + 1) * DE],
                                              c["ident"][:])
                ins.then_inc(turned, 1)

            def hidden_layer(i, u):
                g = UNROLL * i + u
                pe.wait_ge(turned_out, g + 1)
                wait(pe, hidden_ready, g)
                nc.tensor.matmul(ps[:, 3, :], c["eW1s"][:], endsT[:, 0, :], start=True, stop=False)
                nc.tensor.matmul(ps[:, 3, :], c["eW1d"][:], endsT[:, 1, :], start=False, stop=False)
                nc.tensor.matmul(ps[:, 3, :], c["eW1e"][:], edgeT[:], start=False, stop=True).then_inc(hidden_product, 1)

            def message_layer(i, u):
                g = UNROLL * i + u
                pe.wait_ge(hidden_ready, g + 1)
                wait(pe, msg_ready, g)
                nc.tensor.matmul(ps[:, 4, :], c["ones_row"][:], c["eb2"][:].rearrange("o k d -> o (k d)"),
                                 start=True, stop=False, skip_group_check=True)
                for t in range(GT):
                    ins = nc.tensor.matmul(ps[:, 4, t * D:(t + 1) * D], hidden[:, t * P:(t + 1) * P], c["eW2"][:],
                                           start=False, stop=True, skip_group_check=True)
                ins.then_inc(msg_product, 1)

            def add_pairs(i, u):
                g = UNROLL * i + u
                pe.wait_ge(normal_ready, g + 1)
                pe.wait_ge(same_ready, g + 1)
                wait(pe, summedT_ready, g)
                for q in range(2):
                    for s in range(2):
                        t = 2 * q + s
                        ins = nc.tensor.matmul(ps[:, 5, q * 2 * P:(q + 1) * 2 * P],
                                               normal[:, u % 2, t * D:(t + 1) * D], same[:, u % 2, t, :],
                                               start=(s == 0), stop=(s == 1))
                ins.then_inc(pair_product, 1)

            def out_layer(i, u):
                g = UNROLL * i + u
                pe.wait_ge(summedT_ready, g + 1)
                wait(pe, summed_ready, g)
                for t in range(GT):
                    ins = nc.tensor.matmul(ps[:, 6, t * D:(t + 1) * D], summedT[:, t * P:(t + 1) * P], c["nW1m"][:],
                                           start=True, stop=True)
                ins.then_inc(out_product, 1)

            def step(i, u):
                if first(i, u):
                    turn(0, 0)
                m, n = ahead(i, u, -1), ahead(i, u, 1)
                hidden_layer(i, u)
                if m:
                    add_pairs(*m)
                message_layer(i, u)
                if m:
                    out_layer(*m)
                if n:
                    turn(*n)

            sweep(pe, step)
            add_pairs(GROUPS_E // UNROLL, 0)
            out_layer(GROUPS_E // UNROLL, 0)


def output_pass(nc, sb, sem, c, ps, a):
    S = lambda n: sem(f"G_{n}")
    xin = sb("G_xin", [P, UNROLL, NT * D])
    zin = sb("G_zin", [P, UNROLL, NT * D])
    shift = sb("G_shift", [P, NT])
    h = sb("G_h", [P, 2, NT * D])
    zT = sb("G_zT", [P, 2, NT * D])
    v = sb("G_v", [P, NT * D])
    res = sb("G_res", [P, 2, NT * D])
    lx = Stats(sb, sem, "Gx", NT)
    lv = Stats(sb, sem, "Gv", NT)
    loaded = [S(f"loaded{k}") for k in range(UNROLL)]
    stored = [S(f"stored{k}") for k in range(2)]
    shift_ready, h_ready, turned, zT_ready, product = (
        S("shift_ready"), S("h_ready"), S("turned"), S("zT_ready"), S("product"))
    v_ready, normed, scaled, out_ready = S("v_ready"), S("normed"), S("scaled"), S("out_ready")
    tiles = lambda t: t.rearrange("p (k d) -> p k d", d=D)

    with nc.Block() as block:
        @block.sync
        def _(sp):
            def load(i, u):
                g = UNROLL * i + u
                wait(sp, turned, 2 * (g - 3))
                wait(sp, out_ready, g - 3)
                sp.dma_start(xin[:, u, :], rows(a["x2"], node_base(i, u))).then_inc(loaded[u], 16)
                sp.dma_start(zin[:, u, :], rows(a["z3"], node_base(i, u))).then_inc(loaded[u], 16)

            def store(i, u):
                g = UNROLL * i + u
                if isinstance(g, int) and g == GROUPS_N - 1:
                    sp.wait_ge(stored[1 - g % 2], 16 * (g // 2))
                sp.wait_ge(out_ready, g + 1)
                sp.dma_start(rows(a["out"], node_base(i, u)), res[:, u % 2, :]).then_inc(stored[u % 2], 16)

            def step(i, u):
                if first(i, u):
                    for k in range(3):
                        load(0, k)
                m, n = ahead(i, u, -1), ahead(i, u, 3)
                if m:
                    store(*m)
                if n:
                    load(*n)

            sweep(sp, step)
            store(GROUPS_N // UNROLL, 0)
            sp.wait_ge(stored[0], 16 * (GROUPS_N // 2 + 1))
            sp.wait_ge(stored[1], 16 * (GROUPS_N // 2))

        @block.vector
        def _(dve):
            def variances(i, u):
                dve.wait_ge(loaded[u], 32 * (i + 1))
                lx.variances(nc, dve, [xin[:, u, k * D:(k + 1) * D] for k in range(NT)], u % 2, UNROLL * i + u)

            def shifts(i, u):
                g = UNROLL * i + u
                lx.reciprocals(nc, dve, u % 2, g)
                wait(dve, h_ready, g)
                nc.vector.scalar_tensor_tensor(out=shift[:], in0=lx.mean[:, u % 2, :], scalar=-1.0,
                                               in1=lx.rstd[:, u % 2, :], op0=ALU.mult,
                                               op1=ALU.mult).then_inc(shift_ready, 1)

            def updated(i, u):
                g = UNROLL * i + u
                dve.wait_ge(h_ready, g + 1)
                wait(dve, normed, g)
                for half in range(2):
                    cols = slice(half * 512, (half + 1) * 512)
                    dve.wait_ge(product, 2 * g + half + 1)
                    nc.vector.tensor_tensor(v[:, cols], ps[:, 4 + 2 * (u % 2) + half, :], h[:, u % 2, cols],
                                            ALU.add).then_inc(v_ready, 1)
                dve.wait_ge(v_ready, 2 * g + 2)
                lv.variances(nc, dve, [v[:, k * D:(k + 1) * D] for k in range(NT)], u % 2, g)

            def normalise(i, u):
                g = UNROLL * i + u
                lv.reciprocals(nc, dve, u % 2, g)
                wait(dve, stored[u % 2], 16 * (2 * i + u // 2))
                for k in range(NT):
                    cols = slice(k * D, (k + 1) * D)
                    ins = lv.normalise(nc, res[:, u % 2, cols], v[:, cols], k, u % 2)
                ins.then_inc(normed, 1)

            def finish(i, u):
                g = UNROLL * i + u
                dve.wait_ge(scaled, 2 * g + 2)
                nc.vector.tensor_tensor(res[:, u % 2, :], res[:, u % 2, :], xin[:, u, :],
                                        ALU.add).then_inc(out_ready, 1)

            def step(i, u):
                if first(i, u):
                    variances(0, 0)
                    shifts(0, 0)
                m, n = ahead(i, u, -1), ahead(i, u, 1)
                if n:
                    variances(*n)
                updated(i, u)
                if n:
                    shifts(*n)
                if m:
                    finish(*m)
                normalise(i, u)

            sweep(dve, step)
            finish(GROUPS_N // UNROLL, 0)

        @block.gpsimd
        def _(pool):
            def step(i, u):
                g = UNROLL * i + u
                pool.wait_ge(normed, g + 1)
                nc.gpsimd.tensor_tensor(tiles(res[:, u % 2, :]), tiles(res[:, u % 2, :]),
                                        c["ng"][:].unsqueeze(1).broadcast_to([P, NT, D]),
                                        ALU.mult).then_inc(scaled, 1)
                pool.wait_ge(scaled, 2 * g + 1)
                nc.gpsimd.tensor_tensor(tiles(res[:, u % 2, :]), tiles(res[:, u % 2, :]),
                                        c["nbeta"][:].unsqueeze(1).broadcast_to([P, NT, D]),
                                        ALU.add).then_inc(scaled, 1)

            sweep(pool, step)

        @block.scalar
        def _(act):
            def turned_rows(i, u):
                g = UNROLL * i + u
                wait(act, product, 2 * (g - 1))
                for half in range(2):
                    act.wait_ge(turned, 2 * g + half + 1)
                    nc.scalar.activation(zT[:, u % 2, half * 512:(half + 1) * 512], ps[:, 2 * (u % 2) + half, :],
                                         ACT.Relu).then_inc(zT_ready, 1)

            def normal_rows(i, u):
                g = UNROLL * i + u
                act.wait_ge(shift_ready, g + 1)
                wait(act, v_ready, 2 * (g - 1))
                for k in range(NT):
                    cols = slice(k * D, (k + 1) * D)
                    ins = nc.scalar.activation(h[:, u % 2, cols], xin[:, u, cols], ACT.Relu,
                                               bias=shift[:, k:k + 1], scale=lx.rstd[:, u % 2, k:k + 1])
                ins.then_inc(h_ready, 1)

            def step(i, u):
                if first(i, u):
                    lx.deviations(nc, act, c["eps"], 0, 0)
                    normal_rows(0, 0)
                n = ahead(i, u, 1)
                turned_rows(i, u)
                if n:
                    lx.deviations(nc, act, c["eps"], n[1] % 2, UNROLL * n[0] + n[1])
                lv.deviations(nc, act, c["eps"], u % 2, UNROLL * i + u)
                if n:
                    normal_rows(*n)

            sweep(act, step)

        @block.tensor
        def _(pe):
            def turn(i, u):
                g = UNROLL * i + u
                pe.wait_ge(loaded[u], 32 * (i + 1))
                wait(pe, zT_ready, 2 * (g - 1))
                for k in range(NT):
                    ins = nc.tensor.transpose(ps[:, 2 * (u % 2) + k // 4, (k % 4) * P:(k % 4 + 1) * P],
                                              zin[:, u, k * D:(k + 1) * D], c["ident"][:])
                    if k % 4 == 3:
                        ins.then_inc(turned, 1)

            def multiply(i, u):
                g = UNROLL * i + u
                wait(pe, v_ready, 2 * (g - 1))
                for k in range(NT):
                    bank = ps[:, 4 + 2 * (u % 2) + k // 4, :]
                    if k % 4 == 0:
                        pe.wait_ge(zT_ready, 2 * g + k // 4 + 1)
                        nc.tensor.matmul(bank, c["ones_row"][:], c["nb2"][:].rearrange("o k d -> o (k d)"),
                                         start=True, stop=False, skip_group_check=True)
                    ins = nc.tensor.matmul(bank[:, (k % 4) * D:(k % 4 + 1) * D], zT[:, u % 2, k * P:(k + 1) * P],
                                           c["nW2"][:], start=False, stop=True, skip_group_check=True)
                    if k % 4 == 3:
                        ins.then_inc(product, 1)

            def step(i, u):
                if first(i, u):
                    turn(0, 0)
                multiply(i, u)
                n = ahead(i, u, 1)
                if n:
                    turn(*n)

            sweep(pe, step)


def graph_layers(nc, ctx, a, phases=None):
    sb = lambda name, shape, dt=F32: ctx.enter_context(nc.sbuf_tensor(name, shape, dt))
    sem = lambda name: ctx.enter_context(nc.semaphore(name))
    ps = ctx.enter_context(nc.psum_tensor("ps", [P, 8, 512], F32))
    for name in ("z1", "z2", "z3"):
        a[name] = nc.dram_tensor(name, [ROWS_Z, D], F32).ap()
    a["x2"] = nc.dram_tensor("x2", [NODES, D], F32).ap()
    c = setup(nc, sb, sem, a)

    def stage(build, *args, **more):
        with ExitStack() as own:
            own_sb = lambda name, shape, dt=F32: own.enter_context(nc.sbuf_tensor(name, shape, dt))
            build(nc, own_sb, sem, c, ps, *args, **more)

    stage(node_pass, "A", a["x"], a["z1"], c["sl1"], c["b1"], True)
    stage(edge_pass_relational, a, "E1", a["x"], a["z1"], c["w1"], True)
    stage(node_pass, "C", a["z1"], a["z2"], c["sl2"], c["b2"], False)
    stage(edge_pass_relational, a, "E2", a["z1"], a["z2"], c["w2"], False)
    stage(node_pass, "E", a["x"], a["z3"], c["nW1x"], c["nb1"], True, plus=a["z2"], total=a["x2"])
    stage(edge_pass_messages, a)
    stage(output_pass, a)


_WEIGHTS = {
    "w1": "L0_gnn_w1", "sl1": "L0_gnn_sl1", "b1": "L0_gnn_b1", "w2": "L0_gnn_w2", "sl2": "L0_gnn_sl2",
    "b2": "L0_gnn_b2", "eW1": "L1_gnn_eW1", "eb1": "L1_gnn_eb1", "eW2": "L1_gnn_eW2", "eb2": "L1_gnn_eb2",
    "nW1": "L1_gnn_nW1", "nb1": "L1_gnn_nb1", "nW2": "L1_gnn_nW2", "nb2": "L1_gnn_nb2", "eg": "L1_gnn_eg",
    "ebeta": "L1_gnn_ebeta", "ng": "L1_gnn_ng", "nbeta": "L1_gnn_nbeta",
}


def kernel(**inputs):
    import numpy as np
    import concourse.bacc as bacc
    from concourse.bass_utils import run_bass_kernel_spmd

    def padded(a, fill):
        rest = np.full((TILES_E * P - EDGES,) + a.shape[1:], fill, a.dtype)
        return np.concatenate([a, rest])

    src = padded(np.asarray(inputs["src"]), 0)
    dst = padded(np.asarray(inputs["dst"]), PAD_DST)
    laid = {
        "x": np.asarray(inputs["x"]),
        "src": np.ascontiguousarray(src.reshape(TILES_E, P).T),
        "dst": np.ascontiguousarray(dst.reshape(TILES_E, P).T),
        "dst_line": dst,
        "type": padded(np.asarray(inputs["edge_type_8"]), 0),
        "edge": padded(np.asarray(inputs["edge_attr_64"]), 0),
    }
    for name, given in _WEIGHTS.items():
        laid[name] = np.ascontiguousarray(inputs[given])

    nc = bacc.Bacc("TRN2", target_bir_lowering=False, num_devices=1)
    arrays, a = {}, {}
    for name, array in laid.items():
        arrays["in_" + name] = array
        a[name] = nc.dram_tensor("in_" + name, array.shape, mybir.dt.from_np(array.dtype), kind="ExternalInput").ap()
    a["out"] = nc.dram_tensor("out_x", [NODES, D], F32, kind="ExternalOutput").ap()
    with ExitStack() as ctx:
        graph_layers(nc, ctx, a)
    r = run_bass_kernel_spmd(nc, [arrays], core_ids=[0])
    return r.results[0]["out_x"]
```

```python
from contextlib import ExitStack

import concourse.bass as bass
from concourse import mybir

F32 = mybir.dt.float32
I32 = mybir.dt.int32
ALU = mybir.AluOpType
ACT = mybir.ActivationFunctionType

P = 128
D = 128
DE = 64
NREL = 8
EPS = 1e-5

NODES = 50000
EDGES = 25000
TILES_E = 196
GT = 4
GROUPS_E = TILES_E // GT
GE = GT * P
DUMP = NODES
PAD_DST = DUMP + 2 * P
ROWS_S = 50432
NT = 8
GN = NT * P
GROUPS_N = 49
LAST_BASE = NODES - GN

UNROLL = 4
assert GROUPS_E == GROUPS_N == 49
LOOP_END = 11


def sweep(eng, step):
    for u in range(UNROLL):
        step(0, u)
    with eng.Fori(1, LOOP_END) as i:
        for u in range(UNROLL):
            step(i, u)
    for g in range(LOOP_END * UNROLL, GROUPS_N):
        step(g // UNROLL, g % UNROLL)


def ahead(i, u, n):
    v = u + n
    j, w = i + v // UNROLL, v % UNROLL
    if isinstance(j, int) and not 0 <= UNROLL * j + w < GROUPS_N:
        return None
    return j, w


def first(i, u):
    return isinstance(i, int) and i == 0 and u == 0


def wait(eng, sem, value):
    if not (isinstance(value, int) and value <= 0):
        eng.wait_ge(sem, value)


def node_base(i, u):
    g = UNROLL * i + u
    if isinstance(g, int):
        return min(g * GN, LAST_BASE)
    return g * GN


def rows(t, base):
    return t[bass.ds(base, GN), :].rearrange("(p k) d -> p (k d)", p=P)


class Stats:

    def __init__(self, sb, sem, name, n):
        self.n = n
        self.st = sb(name + "_ln_st", [P, n, 6])
        self.small = sb(name + "_ln_small", [P, 4, n])
        self.mean = sb(name + "_ln_mean", [P, 2, n])
        self.var = sb(name + "_ln_var", [P, 2, n])
        self.sd = sb(name + "_ln_sd", [P, n])
        self.rstd = sb(name + "_ln_rstd", [P, 2, n])
        self.shift = sb(name + "_ln_shift", [P, 2, n])
        self.step = sem(name + "_ln_step")
        self.var_ready = sem(name + "_ln_var_ready")
        self.sd_ready = sem(name + "_ln_sd_ready")
        self.rstd_ready = sem(name + "_ln_rstd_ready")
        self.shift_ready = sem(name + "_ln_shift_ready")

    def variances(self, nc, dve, tiles, slot, g, mean=None, var=None):
        st, small = self.st, self.small
        mean = self.mean[:, slot, :] if mean is None else mean
        var = self.var[:, slot, :] if var is None else var
        for k in range(self.n):
            ins = nc.vector.bn_stats(st[:, k, :], tiles[k])
        ins.then_inc(self.step, 1)
        dve.wait_ge(self.step, 3 * g + 1)
        nc.vector.tensor_tensor(small[:, 0, :], st[:, :, 1], st[:, :, 4], ALU.subtract)
        nc.vector.tensor_tensor(small[:, 1, :], st[:, :, 1], st[:, :, 4], ALU.add)
        nc.vector.tensor_tensor(small[:, 2, :], st[:, :, 2], st[:, :, 5], ALU.add).then_inc(self.step, 1)
        dve.wait_ge(self.step, 3 * g + 2)
        nc.vector.tensor_scalar(mean, small[:, 1, :], 0.5, None, ALU.mult)
        nc.vector.scalar_tensor_tensor(out=small[:, 3, :], in0=small[:, 0, :], scalar=D / 4.0,
                                       in1=small[:, 0, :], op0=ALU.mult, op1=ALU.mult).then_inc(self.step, 1)
        dve.wait_ge(self.step, 3 * g + 3)
        nc.vector.tensor_tensor(var, small[:, 3, :], small[:, 2, :],
                                ALU.add).then_inc(self.var_ready, 1)

    def deviations(self, nc, act, eps, slot, g):
        act.wait_ge(self.var_ready, g + 1)
        nc.scalar.activation(self.sd[:], self.var[:, slot, :], ACT.Sqrt, bias=eps[:],
                             scale=1.0 / D).then_inc(self.sd_ready, 1)

    def reciprocals(self, nc, dve, slot, g):
        dve.wait_ge(self.sd_ready, g + 1)
        nc.vector.reciprocal(self.rstd[:, slot, :], self.sd[:]).then_inc(self.rstd_ready, 1)
        dve.wait_ge(self.rstd_ready, g + 1)

    def shifts(self, nc, slot):
        nc.vector.scalar_tensor_tensor(out=self.shift[:, slot, :], in0=self.mean[:, slot, :], scalar=-1.0,
                                       in1=self.rstd[:, slot, :], op0=ALU.mult,
                                       op1=ALU.mult).then_inc(self.shift_ready, 1)

    def scaled(self, nc, out, in_, k, slot, func):
        return nc.scalar.activation(out, in_, func, bias=self.shift[:, slot, k:k + 1],
                                    scale=self.rstd[:, slot, k:k + 1])

    def normalise(self, nc, out, in_, k, slot):
        return nc.vector.tensor_scalar(out, in_, self.mean[:, slot, k:k + 1], self.rstd[:, slot, k:k + 1],
                                       ALU.subtract, ALU.mult)


def zero_rows(eng, zeros, s, base, done):
    eng.dma_start(rows(s, base), zeros[:]).then_inc(done, 16)


def setup(nc, sb, sem, a):
    c = {}

    def keep(name, shape, dt=F32):
        c[name] = sb("c_" + name, shape, dt)
        return c[name]

    ident = keep("ident", [P, P])
    earlier = keep("earlier", [P, 2, 2 * P])
    eps = keep("eps", [P, 1])
    zeros = keep("zeros", [P, NT * D])
    ones_row = keep("ones_row", [1, P])
    src = keep("src", [P, TILES_E], I32)
    dst = keep("dst", [P, TILES_E], I32)
    dstf = keep("dstf", [P, TILES_E])
    dump_less_dst = keep("dump_less_dst", [P, TILES_E])
    keep("scat", [P, TILES_E], I32)
    dump = keep("dump", [P, TILES_E])
    for name in ("x2_mean", "x2_var", "x2_rstd", "x2_shift"):
        keep(name, [P, GROUPS_N * NT])

    loads = [(src[:], a["src"]), (dst[:], a["dst"])]
    for name in ("w1", "w2"):
        loads.append((keep(name, [P, NREL, D])[:], a[name].rearrange("r d f -> d r f")))
    for name in ("sl1", "sl2", "eW2", "nW2"):
        loads.append((keep(name, [P, D])[:], a[name]))
    loads.append((keep("eW1s", [P, D])[:], a["eW1"][0:D, :]))
    loads.append((keep("eW1d", [P, D])[:], a["eW1"][D:2 * D, :]))
    loads.append((keep("eW1e", [DE, D])[:], a["eW1"][2 * D:2 * D + DE, :]))
    loads.append((keep("nW1x", [P, D])[:], a["nW1"][0:D, :]))
    loads.append((keep("nW1m", [P, D])[:], a["nW1"][D:2 * D, :]))
    for name in ("b1", "b2", "nb2", "eg", "ebeta", "ng", "nbeta"):
        loads.append((keep(name, [P, D])[:], a[name].partition_broadcast(P)))
    for name in ("eb1", "nb1"):
        loads.append((keep(name, [P, 1])[:], a[name].unsqueeze(1)))
    t = keep("eb2", [1, 4, D])
    for k in range(4):
        loads.append((t[0:1, k, :], a["eb2"].unsqueeze(0)))

    loaded, pool_done, dve_done = sem("loaded"), sem("pool_done"), sem("dve_done")
    c["s1_zeroed"] = [sem(f"s1_zeroed{k}") for k in range(4)]
    with nc.Block() as block:
        @block.sync
        def _(sp):
            for out, in_ in loads:
                sp.dma_start(out, in_).then_inc(loaded, 16)
            sp.wait_ge(loaded, 16 * len(loads))

        @block.vector
        def _(dve):
            nc.vector.memset(zeros[:], 0.0).then_inc(dve_done, 1)
            nc.vector.memset(eps[:], EPS)
            nc.vector.memset(ones_row[:], 1.0)
            dve.wait_ge(loaded, 16 * len(loads))
            nc.vector.tensor_copy(dstf[:], dst[:]).then_inc(dve_done, 1)
            dve.wait_ge(dve_done, 2)
            dve.wait_ge(pool_done, 5)
            nc.vector.tensor_tensor(dump_less_dst[:], dump[:], dstf[:], ALU.subtract)

        @block.gpsimd
        def _(pool):
            nc.gpsimd.memset(ident[:], 0.0).then_inc(pool_done, 1)
            nc.gpsimd.memset(earlier[:], 1.0).then_inc(pool_done, 1)
            pool.wait_ge(pool_done, 2)
            nc.gpsimd.affine_select(out=ident[:], in_=ident[:], compare_op=ALU.not_equal, fill=1.0, base=0,
                                    pattern=[[-1, P]], channel_multiplier=1).then_inc(pool_done, 1)
            nc.gpsimd.affine_select(out=earlier[:], in_=earlier[:], compare_op=ALU.is_gt, fill=0.0, base=0,
                                    pattern=[[P, 2], [-1, 2 * P]], channel_multiplier=1).then_inc(pool_done, 1)
            nc.gpsimd.iota(dump[:], pattern=[[0, TILES_E // 2], [P, 2]], base=DUMP, channel_multiplier=1,
                           allow_small_or_imprecise_dtypes=True).then_inc(pool_done, 1)
            pool.wait_ge(pool_done, 5)
    return c


def last_store(sp, stored, g):
    if isinstance(g, int) and g == GROUPS_N - 1:
        sp.wait_ge(stored[1 - g % 2], 16 * (g // 2))


def all_stored(sp, stored):
    sp.wait_ge(stored[0], 16 * (GROUPS_N // 2 + 1))
    sp.wait_ge(stored[1], 16 * (GROUPS_N // 2))


def tiles_of(t):
    return t.rearrange("p (k d) -> p k d", d=D)


def each_tile(row, n):
    return row[:].unsqueeze(1).broadcast_to([P, n, D])


def node_pass_1(nc, sb, sem, c, ps, a):
    S = lambda n: sem(f"N1_{n}")
    ON_ACT = 3
    xin = sb("N1_xin", [P, UNROLL, NT * D])
    sin = sb("N1_sin", [P, UNROLL, NT * D])
    hT = sb("N1_hT", [P, 2, NT * D])
    y = sb("N1_y", [P, 2, NT * D])
    ln = Stats(sb, sem, "N1", NT)
    loaded = [S(f"loaded{k}") for k in range(UNROLL)]
    stored = [S(f"stored{k}") for k in range(2)]
    biased, normed, act_normed, turned = S("biased"), S("normed"), S("act_normed"), S("turned")
    hT_ready, product, y_ready = S("hT_ready"), S("product"), S("y_ready")

    with nc.Block() as block:
        @block.sync
        def _(sp):
            def load(i, u):
                g = UNROLL * i + u
                wait(sp, product, 2 * (g - 3))
                sp.dma_start(xin[:, u, :], rows(a["x"], node_base(i, u))).then_inc(loaded[u], 16)
                sp.dma_start(sin[:, u, :], rows(a["s1"], node_base(i, u))).then_inc(loaded[u], 16)

            def step(i, u):
                g = UNROLL * i + u
                if first(i, u):
                    for k in range(3):
                        load(0, k)
                n = ahead(i, u, 3)
                if n:
                    load(*n)
                last_store(sp, stored, g)
                sp.wait_ge(y_ready, 2 * g + 2)
                sp.dma_start(rows(a["y1"], node_base(i, u)), y[:, u % 2, :]).then_inc(stored[u % 2], 16)

            sweep(sp, step)
            all_stored(sp, stored)

        @block.gpsimd
        def _(pool):
            def step(i, u):
                pool.wait_ge(loaded[u], 32 * (i + 1))
                nc.gpsimd.tensor_tensor(tiles_of(sin[:, u, :]), tiles_of(sin[:, u, :]), each_tile(c["b1"], NT),
                                        ALU.add).then_inc(biased, 1)

            sweep(pool, step)

        @block.vector
        def _(dve):
            def variances(i, u):
                dve.wait_ge(loaded[u], 32 * (i + 1))
                ln.variances(nc, dve, [xin[:, u, k * D:(k + 1) * D] for k in range(NT)], u % 2, UNROLL * i + u)

            def normalise(i, u):
                g = UNROLL * i + u
                ln.reciprocals(nc, dve, u % 2, g)
                ln.shifts(nc, u % 2)
                for k in range(NT - ON_ACT):
                    tile = xin[:, u, k * D:(k + 1) * D]
                    ins = ln.normalise(nc, tile, tile, k, u % 2)
                ins.then_inc(normed, 1)

            def step(i, u):
                for k in range(2 if first(i, u) else 0):
                    variances(0, k)
                    normalise(0, k)
                n = ahead(i, u, 2)
                if n:
                    wait(dve, act_normed, UNROLL * n[0] + n[1] - 1)
                    variances(*n)
                    normalise(*n)

            sweep(dve, step)

        @block.scalar
        def _(act):
            def normalise(i, u):
                g = UNROLL * i + u
                act.wait_ge(ln.shift_ready, g + 1)
                for k in range(NT - ON_ACT, NT):
                    tile = xin[:, u, k * D:(k + 1) * D]
                    ins = ln.scaled(nc, tile, tile, k, u % 2, ACT.Identity)
                ins.then_inc(act_normed, 1)

            def turned_rows(i, u):
                g = UNROLL * i + u
                wait(act, product, 2 * (g - 1))
                for h in range(2):
                    act.wait_ge(turned, 2 * g + h + 1)
                    nc.scalar.activation(hT[:, u % 2, h * 512:(h + 1) * 512], ps[:, 2 * (u % 2) + h, :],
                                         ACT.Relu).then_inc(hT_ready, 1)

            def results(i, u):
                g = UNROLL * i + u
                wait(act, stored[u % 2], 16 * (2 * i + u // 2))
                for h in range(2):
                    act.wait_ge(product, 2 * g + h + 1)
                    nc.scalar.activation(y[:, u % 2, h * 512:(h + 1) * 512], ps[:, 4 + 2 * (u % 2) + h, :],
                                         ACT.Relu).then_inc(y_ready, 1)

            def step(i, u):
                if first(i, u):
                    for k in range(2):
                        ln.deviations(nc, act, c["eps"], k, k)
                        normalise(0, k)
                    turned_rows(0, 0)
                m, n = ahead(i, u, 1), ahead(i, u, 2)
                if m:
                    turned_rows(*m)
                if n:
                    ln.deviations(nc, act, c["eps"], n[1] % 2, UNROLL * n[0] + n[1])
                    normalise(*n)
                results(i, u)

            sweep(act, step)

        @block.tensor
        def _(pe):
            def turn(i, u):
                g = UNROLL * i + u
                pe.wait_ge(normed, g + 1)
                pe.wait_ge(act_normed, g + 1)
                wait(pe, hT_ready, 2 * (g - 1))
                for k in range(NT):
                    ins = nc.tensor.transpose(ps[:, 2 * (u % 2) + k // 4, (k % 4) * P:(k % 4 + 1) * P],
                                              xin[:, u, k * D:(k + 1) * D], c["ident"][:])
                    if k % 4 == 3:
                        ins.then_inc(turned, 1)

            def multiply(i, u):
                g = UNROLL * i + u
                pe.wait_ge(biased, g + 1)
                wait(pe, y_ready, 2 * (g - 1))
                for h in range(2):
                    bank = ps[:, 4 + 2 * (u % 2) + h, :]
                    nc.tensor.matmul(bank, c["ident"][:], sin[:, u, h * 512:(h + 1) * 512],
                                     start=True, stop=False, skip_group_check=True)
                    pe.wait_ge(hT_ready, 2 * g + h + 1)
                    for k in range(4):
                        at = h * 512 + k * P
                        ins = nc.tensor.matmul(bank[:, k * D:(k + 1) * D], hT[:, u % 2, at:at + P], c["sl1"][:],
                                               start=False, stop=True, skip_group_check=True)
                    ins.then_inc(product, 1)

            def step(i, u):
                if first(i, u):
                    turn(0, 0)
                n = ahead(i, u, 1)
                if n:
                    turn(*n)
                multiply(i, u)

            sweep(pe, step)


def node_pass_2(nc, sb, sem, c, ps, a):
    S = lambda n: sem(f"N2_{n}")
    yin = sb("N2_yin", [P, UNROLL, NT * D])
    sin = sb("N2_sin", [P, UNROLL, NT * D])
    xin = sb("N2_xin", [P, UNROLL, NT * D])
    yT = sb("N2_yT", [P, 2, NT * D])
    x2 = sb("N2_x2", [P, 2, NT * D])
    sd = sb("N2_sd", [P, GROUPS_N * NT])
    ln = Stats(sb, sem, "N2", NT)
    loaded = [S(f"loaded{k}") for k in range(UNROLL)]
    stored = [S(f"stored{k}") for k in range(2)]
    biased, turned, yT_ready, product, x2_ready, all_rstd = (
        S("biased"), S("turned"), S("yT_ready"), S("product"), S("x2_ready"), S("all_rstd"))

    with nc.Block() as block:
        @block.sync
        def _(sp):
            def load(i, u):
                g = UNROLL * i + u
                wait(sp, x2_ready, 2 * (g - 3))
                for slots, t in ((yin, "y1"), (sin, "s2"), (xin, "x")):
                    sp.dma_start(slots[:, u, :], rows(a[t], node_base(i, u))).then_inc(loaded[u], 16)

            def step(i, u):
                g = UNROLL * i + u
                if first(i, u):
                    for k in range(3):
                        load(0, k)
                n = ahead(i, u, 3)
                if n:
                    load(*n)
                last_store(sp, stored, g)
                sp.wait_ge(x2_ready, 2 * g + 2)
                sp.dma_start(rows(a["x2"], node_base(i, u)), x2[:, u % 2, :]).then_inc(stored[u % 2], 16)

            sweep(sp, step)
            all_stored(sp, stored)

        @block.gpsimd
        def _(pool):
            def step(i, u):
                pool.wait_ge(loaded[u], 48 * (i + 1))
                nc.gpsimd.tensor_tensor(tiles_of(sin[:, u, :]), tiles_of(sin[:, u, :]), each_tile(c["b2"], NT),
                                        ALU.add).then_inc(biased, 1)

            sweep(pool, step)

        @block.vector
        def _(dve):
            def step(i, u):
                g = UNROLL * i + u
                wait(dve, stored[u % 2], 16 * (2 * i + u // 2))
                dve.wait_ge(loaded[u], 48 * (i + 1))
                for h in range(2):
                    half = slice(h * 512, (h + 1) * 512)
                    dve.wait_ge(product, 2 * g + h + 1)
                    nc.vector.scalar_tensor_tensor(out=x2[:, u % 2, half], in0=ps[:, 4 + 2 * (u % 2) + h, :],
                                                   scalar=0.0, in1=xin[:, u, half], op0=ALU.max,
                                                   op1=ALU.add).then_inc(x2_ready, 1)
                dve.wait_ge(x2_ready, 2 * g + 2)
                here = bass.ds(g * NT, NT)
                ln.variances(nc, dve, [x2[:, u % 2, k * D:(k + 1) * D] for k in range(NT)], u % 2, g,
                             c["x2_mean"][:, here], c["x2_var"][:, here])

            sweep(dve, step)
            dve.wait_ge(ln.sd_ready, 1)
            nc.vector.reciprocal(c["x2_rstd"][:], sd[:]).then_inc(all_rstd, 1)
            dve.wait_ge(all_rstd, 1)
            nc.vector.scalar_tensor_tensor(out=c["x2_shift"][:], in0=c["x2_mean"][:], scalar=-1.0,
                                           in1=c["x2_rstd"][:], op0=ALU.mult, op1=ALU.mult)

        @block.scalar
        def _(act):
            def step(i, u):
                g = UNROLL * i + u
                wait(act, product, 2 * (g - 1))
                for h in range(2):
                    act.wait_ge(turned, 2 * g + h + 1)
                    nc.scalar.copy(yT[:, u % 2, h * 512:(h + 1) * 512],
                                   ps[:, 2 * (u % 2) + h, :]).then_inc(yT_ready, 1)

            sweep(act, step)
            act.wait_ge(ln.var_ready, GROUPS_N)
            nc.scalar.activation(sd[:], c["x2_var"][:], ACT.Sqrt, bias=c["eps"][:],
                                 scale=1.0 / D).then_inc(ln.sd_ready, 1)

        @block.tensor
        def _(pe):
            def turn(i, u):
                g = UNROLL * i + u
                pe.wait_ge(loaded[u], 48 * (i + 1))
                wait(pe, yT_ready, 2 * (g - 1))
                for k in range(NT):
                    ins = nc.tensor.transpose(ps[:, 2 * (u % 2) + k // 4, (k % 4) * P:(k % 4 + 1) * P],
                                              yin[:, u, k * D:(k + 1) * D], c["ident"][:])
                    if k % 4 == 3:
                        ins.then_inc(turned, 1)

            def multiply(i, u):
                g = UNROLL * i + u
                pe.wait_ge(biased, g + 1)
                wait(pe, x2_ready, 2 * (g - 1))
                for h in range(2):
                    bank = ps[:, 4 + 2 * (u % 2) + h, :]
                    nc.tensor.matmul(bank, c["ident"][:], sin[:, u, h * 512:(h + 1) * 512],
                                     start=True, stop=False, skip_group_check=True)
                    pe.wait_ge(yT_ready, 2 * g + h + 1)
                    for k in range(4):
                        at = h * 512 + k * P
                        ins = nc.tensor.matmul(bank[:, k * D:(k + 1) * D], yT[:, u % 2, at:at + P], c["sl2"][:],
                                               start=False, stop=True, skip_group_check=True)
                    ins.then_inc(product, 1)

            def step(i, u):
                if first(i, u):
                    turn(0, 0)
                multiply(i, u)
                n = ahead(i, u, 1)
                if n:
                    turn(*n)

            sweep(pe, step)


def node_pass_3(nc, sb, sem, c, ps, a):
    S = lambda n: sem(f"N3_{n}")
    ON_ACT = 2
    xin = sb("N3_xin", [P, UNROLL, NT * D])
    sin = sb("N3_sin", [P, UNROLL, NT * D])
    base = sb("N3_base", [P, UNROLL, NT * D])
    h = sb("N3_h", [P, 2, NT * D])
    hb = sb("N3_hb", [P, 2, NT * D])
    hT = sb("N3_hT", [P, NT * D])
    hidT = sb("N3_hidT", [P, NT * D])
    v = sb("N3_v", [P, NT * D])
    res = sb("N3_res", [P, UNROLL, NT * D])
    ln = Stats(sb, sem, "N3", NT)
    loaded = [S(f"loaded{k}") for k in range(UNROLL)]
    stored = [S(f"stored{k}") for k in range(UNROLL)]
    h_ready, turned, hT_ready, hidden, hidT_ready, product = (
        S("h_ready"), S("turned"), S("hT_ready"), S("hidden"), S("hidT_ready"), S("product"))
    base_ready, hb_ready, v_ready, normed, act_normed, scaled, out_ready = (
        S("base_ready"), S("hb_ready"), S("v_ready"), S("normed"), S("act_normed"), S("scaled"), S("out_ready"))

    with nc.Block() as block:
        @block.sync
        def _(sp):
            def load(i, u):
                g = UNROLL * i + u
                wait(sp, hidden, 2 * (g - 3))
                wait(sp, h_ready, g - 3)
                wait(sp, base_ready, g - 3)
                sp.dma_start(xin[:, u, :], rows(a["x2"], node_base(i, u))).then_inc(loaded[u], 16)
                sp.dma_start(sin[:, u, :], rows(a["s3"], node_base(i, u))).then_inc(loaded[u], 16)

            def store(i, u):
                g = UNROLL * i + u
                if isinstance(g, int) and g == GROUPS_N - 1:
                    sp.wait_ge(stored[(g - 1) % UNROLL], 16 * (g // UNROLL))
                sp.wait_ge(out_ready, g + 1)
                sp.dma_start(rows(a["out"], node_base(i, u)), res[:, u, :]).then_inc(stored[u], 16)

            def step(i, u):
                if first(i, u):
                    for k in range(3):
                        load(0, k)
                m, n = ahead(i, u, -2), ahead(i, u, 3)
                if n:
                    load(*n)
                if m:
                    store(*m)

            sweep(sp, step)
            for g in (GROUPS_N - 2, GROUPS_N - 1):
                store(g // UNROLL, g % UNROLL)
            for k in range(UNROLL):
                sp.wait_ge(stored[k], 16 * ((GROUPS_N - 1 - k) // UNROLL + 1))

        @block.scalar
        def _(act):
            def rows_h(i, u):
                g = UNROLL * i + u
                act.wait_ge(loaded[u], 32 * (i + 1))
                wait(act, turned, 2 * (g - 1))
                wait(act, hb_ready, g - 1)
                for k in range(NT):
                    cols = slice(k * D, (k + 1) * D)
                    at = bass.ds(g * NT + k, 1)
                    ins = nc.scalar.activation(h[:, u % 2, cols], xin[:, u, cols], ACT.Relu,
                                               bias=c["x2_shift"][:, at], scale=c["x2_rstd"][:, at])
                ins.then_inc(h_ready, 1)

            def turned_rows(i, u):
                g = UNROLL * i + u
                wait(act, hidden, 2 * g)
                for half in range(2):
                    act.wait_ge(turned, 2 * g + half + 1)
                    nc.scalar.copy(hT[:, half * 512:(half + 1) * 512], ps[:, half, :]).then_inc(hT_ready, 1)

            def hidden_rows(i, u):
                g = UNROLL * i + u
                wait(act, product, 2 * g)
                for half in range(2):
                    act.wait_ge(hidden, 2 * g + half + 1)
                    nc.scalar.activation(hidT[:, half * 512:(half + 1) * 512], ps[:, 2 + half, :], ACT.Relu,
                                         bias=c["nb1"][:]).then_inc(hidT_ready, 1)

            def outer_norm(i, u):
                g = UNROLL * i + u
                act.wait_ge(ln.shift_ready, g + 1)
                wait(act, stored[u], 16 * i)
                for k in range(NT - ON_ACT, NT):
                    cols = slice(k * D, (k + 1) * D)
                    ins = ln.scaled(nc, res[:, u, cols], v[:, cols], k, u % 2, ACT.Identity)
                ins.then_inc(act_normed, 1)

            def step(i, u):
                if first(i, u):
                    rows_h(0, 0)
                    turned_rows(0, 0)
                m, n = ahead(i, u, -1), ahead(i, u, 1)
                if n:
                    rows_h(*n)
                hidden_rows(i, u)
                if m:
                    ln.deviations(nc, act, c["eps"], m[1] % 2, UNROLL * m[0] + m[1])
                if n:
                    turned_rows(*n)
                if m:
                    outer_norm(*m)

            sweep(act, step)
            ln.deviations(nc, act, c["eps"], 0, GROUPS_N - 1)
            outer_norm(GROUPS_N // UNROLL, 0)

        @block.tensor
        def _(pe):
            def turn(i, u):
                g = UNROLL * i + u
                pe.wait_ge(h_ready, g + 1)
                wait(pe, hT_ready, 2 * g)
                for k in range(NT):
                    ins = nc.tensor.transpose(ps[:, k // 4, (k % 4) * P:(k % 4 + 1) * P],
                                              h[:, u % 2, k * D:(k + 1) * D], c["ident"][:])
                    if k % 4 == 3:
                        ins.then_inc(turned, 1)

            def hidden_layer(i, u):
                g = UNROLL * i + u
                pe.wait_ge(loaded[u], 32 * (i + 1))
                for half in range(2):
                    pe.wait_ge(hT_ready, 2 * g + half + 1)
                    wait(pe, hidT_ready, 2 * (g - 1) + half + 1)
                    bank = ps[:, 2 + half, :]
                    nc.tensor.matmul(bank, c["nW1x"][:], hT[:, half * 512:(half + 1) * 512],
                                     start=True, stop=False, skip_group_check=True)
                    for k in range(4):
                        at = half * 512 + k * D
                        ins = nc.tensor.matmul(bank[:, k * P:(k + 1) * P], sin[:, u, at:at + D], c["ident"][:],
                                               start=False, stop=True, skip_group_check=True)
                    ins.then_inc(hidden, 1)

            def output_layer(i, u):
                g = UNROLL * i + u
                wait(pe, v_ready, 2 * (g - 1))
                for half in range(2):
                    pe.wait_ge(hidT_ready, 2 * g + half + 1)
                    for k in range(4):
                        at = half * 512 + k * P
                        ins = nc.tensor.matmul(ps[:, 4 + 2 * (u % 2) + half, k * D:(k + 1) * D],
                                               hidT[:, at:at + P], c["nW2"][:], start=True, stop=True)
                    ins.then_inc(product, 1)

            def step(i, u):
                if first(i, u):
                    turn(0, 0)
                hidden_layer(i, u)
                n = ahead(i, u, 1)
                if n:
                    turn(*n)
                output_layer(i, u)

            sweep(pe, step)

        @block.gpsimd
        def _(pool):
            def bases(i, u):
                g = UNROLL * i + u
                pool.wait_ge(loaded[u], 32 * (i + 1))
                wait(pool, out_ready, g - 3)
                nc.gpsimd.tensor_tensor(tiles_of(base[:, u, :]), tiles_of(xin[:, u, :]), each_tile(c["nbeta"], NT),
                                        ALU.add).then_inc(base_ready, 1)

            def biased(i, u):
                g = UNROLL * i + u
                pool.wait_ge(h_ready, g + 1)
                wait(pool, v_ready, 2 * (g - 1))
                nc.gpsimd.tensor_tensor(tiles_of(hb[:, u % 2, :]), tiles_of(h[:, u % 2, :]), each_tile(c["nb2"], NT),
                                        ALU.add).then_inc(hb_ready, 1)

            def scale(i, u):
                g = UNROLL * i + u
                pool.wait_ge(normed, g + 1)
                pool.wait_ge(act_normed, g + 1)
                nc.gpsimd.tensor_tensor(tiles_of(res[:, u, :]), tiles_of(res[:, u, :]), each_tile(c["ng"], NT),
                                        ALU.mult).then_inc(scaled, 1)

            def step(i, u):
                if first(i, u):
                    bases(0, 0)
                m, n = ahead(i, u, -2), ahead(i, u, 1)
                biased(i, u)
                if m:
                    scale(*m)
                if n:
                    bases(*n)

            sweep(pool, step)
            for g in (GROUPS_N - 2, GROUPS_N - 1):
                scale(g // UNROLL, g % UNROLL)

        @block.vector
        def _(dve):
            def updated(i, u):
                g = UNROLL * i + u
                dve.wait_ge(hb_ready, g + 1)
                wait(dve, normed, g)
                wait(dve, act_normed, g)
                for half in range(2):
                    cols = slice(half * 512, (half + 1) * 512)
                    dve.wait_ge(product, 2 * g + half + 1)
                    nc.vector.tensor_tensor(v[:, cols], ps[:, 4 + 2 * (u % 2) + half, :], hb[:, u % 2, cols],
                                            ALU.add).then_inc(v_ready, 1)
                dve.wait_ge(v_ready, 2 * g + 2)
                ln.variances(nc, dve, [v[:, k * D:(k + 1) * D] for k in range(NT)], u % 2, g)

            def normalise(i, u):
                g = UNROLL * i + u
                ln.reciprocals(nc, dve, u % 2, g)
                ln.shifts(nc, u % 2)
                wait(dve, stored[u], 16 * i)
                for k in range(NT - ON_ACT):
                    cols = slice(k * D, (k + 1) * D)
                    ins = ln.normalise(nc, res[:, u, cols], v[:, cols], k, u % 2)
                ins.then_inc(normed, 1)

            def finish(i, u):
                g = UNROLL * i + u
                dve.wait_ge(scaled, g + 1)
                nc.vector.tensor_tensor(res[:, u, :], res[:, u, :], base[:, u, :], ALU.add).then_inc(out_ready, 1)

            def step(i, u):
                m, l = ahead(i, u, -1), ahead(i, u, -2)
                if m:
                    updated(*m)
                if l:
                    finish(*l)
                if m:
                    normalise(*m)

            sweep(dve, step)
            updated(GROUPS_N // UNROLL, 0)
            finish((GROUPS_N - 2) // UNROLL, (GROUPS_N - 2) % UNROLL)
            normalise(GROUPS_N // UNROLL, 0)
            finish(GROUPS_N // UNROLL, 0)


def edge_pass_relational(nc, sb, sem, c, ps, a, name, x, s, w, norm):
    S = lambda n: sem(f"{name}_{n}")
    xg = sb(f"{name}_xg", [P, UNROLL, GE])
    src_ring = sb(f"{name}_src_ring", [P, UNROLL, GT], I32)
    scat_ring = sb(f"{name}_scat_ring", [P, UNROLL, GT], I32)
    type_row = sb(f"{name}_type_row", [P, UNROLL, GE], I32)
    dst_row = sb(f"{name}_dst_row", [P, UNROLL, GE], I32)
    hT = sb(f"{name}_hT", [P, 2, GE])
    masked = sb(f"{name}_masked", [P, 2, NREL, GE])
    msg = sb(f"{name}_msg", [P, 2, GE])
    same = sb(f"{name}_same", [P, 2, GT, 2 * P])
    summed = sb(f"{name}_summed", [P, 2, GE])
    ln = Stats(sb, sem, name, GT) if norm else None
    if norm:
        before = sb(f"{name}_before", [P, 2 * P])
        count = sb(f"{name}_count", [P, GT])
        shift = sb(f"{name}_move", [P, GT])
        scat_step, zeroed = S("scat_step"), S("zeroed")
    gathered = [S(f"gathered{k}") for k in range(UNROLL)]
    rows_in = [S(f"rows_in{k}") for k in range(UNROLL)]
    src_ready, scat_ready, added, issuing = S("src_ready"), S("scat_ready"), S("added"), S("issuing")
    normed, turned, hT_ready, mask_ready = S("normed"), S("turned"), S("hT_ready"), S("mask_ready")
    product, msg_ready, same_ready = S("product"), S("msg_ready"), S("same_ready")
    pair_product, summed_ready = S("pair_product"), S("summed_ready")

    def zero_first_sums(sp):
        whole = ROWS_S // GN
        for g in range(whole):
            wait(sp, c["s1_zeroed"][g % 4], 16 * (g // 4))
            zero_rows(sp, c["zeros"], s, g * GN, c["s1_zeroed"][g % 4])
        sp.dma_start(s[whole * GN:ROWS_S, :].rearrange("(p k) d -> p (k d)", p=P),
                     c["zeros"][:, 0:ROWS_S % GN // P * D]).then_inc(c["s1_zeroed"][whole % 4], 16)

    with nc.Block() as block:
        @block.sync
        def _(sp):
            def load(i, u):
                g = UNROLL * i + u
                wait(sp, scat_ready, g - 3)
                edges = bass.ds(g * GE, GE)
                sp.dma_start(type_row[:, u, :], a["type"][edges].partition_broadcast(P)).then_inc(rows_in[u], 16)
                sp.dma_start(dst_row[:, u, :], a["dst_line"][edges].partition_broadcast(P)).then_inc(rows_in[u], 16)

            def step(i, u):
                if first(i, u):
                    for k in range(3):
                        load(0, k)
                    if norm:
                        zero_first_sums(sp)
                n = ahead(i, u, 3)
                if n:
                    load(*n)
                if norm:
                    for k, t in enumerate(("s2", "s3")):
                        zero_rows(sp, c["zeros"], a[t], (UNROLL * i + u) * GN, zeroed)

            sweep(sp, step)
            if norm:
                rest = GROUPS_N * GN
                for t in ("s2", "s3"):
                    sp.dma_start(a[t][rest:ROWS_S, :].rearrange("(p k) d -> p (k d)", p=P),
                                 c["zeros"][:, 0:(ROWS_S - rest) // P * D]).then_inc(zeroed, 16)
                sp.wait_ge(zeroed, 16 * 2 * (GROUPS_N + 1))

        @block.gpsimd
        def _(pool):
            def gather(i, u, q):
                g = UNROLL * i + u
                if q == 0:
                    pool.wait_ge(src_ready, g + 1)
                    wait(pool, turned, g - 3)
                    pool.sem_inc(issuing, 1)
                for t in (2 * q, 2 * q + 1):
                    pool.indirect_dma_start(
                        xg[:, u, t * D:(t + 1) * D], None, x,
                        bass.IndirectOffsetOnAxis(ap=src_ring[:, u, t:t + 1], axis=0)).then_inc(gathered[u], 16)

            def scatter(i, u, q):
                g = UNROLL * i + u
                if norm and isinstance(g, int) and g == 0 and q == 0:
                    for k in range(4):
                        pool.wait_ge(c["s1_zeroed"][k], 16 * ((ROWS_S // GN - k) // 4 + 1))
                if q == 0:
                    pool.wait_ge(summed_ready, g + 1)
                    pool.wait_ge(scat_ready, g + 1)
                wait(pool, added, 32 * (2 * g + q))
                pool.sem_inc(issuing, 1)
                for t in (2 * q, 2 * q + 1):
                    pool.indirect_dma_start(
                        s, bass.IndirectOffsetOnAxis(ap=scat_ring[:, u, t:t + 1], axis=0),
                        summed[:, u % 2, t * D:(t + 1) * D], None, compute_op=ALU.add).then_inc(added, 16)

            def step(i, u):
                if first(i, u):
                    for k in range(3):
                        gather(0, k, 0)
                        gather(0, k, 1)
                n, m = ahead(i, u, 3), ahead(i, u, -2)
                for q in range(2):
                    if n:
                        gather(*n, q)
                    if m:
                        scatter(*m, q)

            sweep(pool, step)
            for g in (GROUPS_E - 2, GROUPS_E - 1):
                scatter(g // UNROLL, g % UNROLL, 0)
                scatter(g // UNROLL, g % UNROLL, 1)
            pool.wait_ge(added, 64 * GROUPS_E)

        @block.vector
        def _(dve):
            def sources(i, u):
                g = UNROLL * i + u
                wait(dve, gathered[u], 64 * i)
                nc.vector.tensor_scalar(src_ring[:, u, :], c["src"][:, bass.ds(g * GT, GT)], 0.0, None, ALU.add).then_inc(src_ready, 1)

            def variances(i, u):
                dve.wait_ge(gathered[u], 64 * (i + 1))
                wait(dve, normed, UNROLL * i + u - 1)
                ln.variances(nc, dve, [xg[:, u, t * D:(t + 1) * D] for t in range(GT)], u % 2, UNROLL * i + u)

            def shifts(i, u):
                g = UNROLL * i + u
                ln.reciprocals(nc, dve, u % 2, g)
                ln.shifts(nc, u % 2)

            def masks(i, u):
                g = UNROLL * i + u
                dve.wait_ge(rows_in[u], 32 * (i + 1))
                dve.wait_ge(hT_ready, g + 1)
                wait(dve, product, g - 1)
                for r in range(NREL):
                    nc.vector.scalar_tensor_tensor(out=masked[:, u % 2, r, :], in0=type_row[:, u, :],
                                                   scalar=float(r), in1=hT[:, u % 2, :],
                                                   op0=ALU.is_equal, op1=ALU.mult).then_inc(mask_ready, 1)

            def equalities(i, u):
                g = UNROLL * i + u
                wait(dve, pair_product, g - 1)
                for t in range(GT):
                    pair = slice(t // 2 * 2 * P, (t // 2 + 1) * 2 * P)
                    ins = nc.vector.tensor_scalar(same[:, u % 2, t, :], dst_row[:, u, pair],
                                                  c["dstf"][:, bass.ds(g * GT + t, 1)], None, ALU.is_equal)
                    if norm:
                        wait(dve, scat_step, 6 * g + t)
                        nc.vector.scalar_tensor_tensor(
                            out=before[:], in0=dst_row[:, u, pair], scalar=c["dstf"][:, bass.ds(g * GT + t, 1)],
                            in1=c["earlier"][:, t % 2, :], op0=ALU.is_equal, op1=ALU.mult,
                            accum_out=count[:, t:t + 1]).then_inc(scat_step, 1)
                ins.then_inc(same_ready, 1)

            def scatter_rows(i, u):
                g = UNROLL * i + u
                here = bass.ds(g * GT, GT)
                if norm:
                    dve.wait_ge(scat_step, 6 * g + 4)
                    nc.vector.scalar_tensor_tensor(out=shift[:], in0=count[:], scalar=1.0,
                                                   in1=c["dump_less_dst"][:, here],
                                                   op0=ALU.min, op1=ALU.mult).then_inc(scat_step, 1)
                    dve.wait_ge(scat_step, 6 * g + 5)
                    nc.vector.tensor_tensor(c["scat"][:, here], shift[:], c["dstf"][:, here],
                                            ALU.add).then_inc(scat_step, 1)
                    dve.wait_ge(scat_step, 6 * g + 6)
                wait(dve, added, 64 * (g - 3))
                nc.vector.tensor_scalar(scat_ring[:, u, :], c["scat"][:, here], 0.0, None, ALU.add).then_inc(scat_ready, 1)

            def step(i, u):
                if first(i, u):
                    for k in range(UNROLL):
                        sources(0, k)
                    for k in range(2 if norm else 0):
                        variances(0, k)
                        shifts(0, k)
                    masks(0, 0)
                m, n = ahead(i, u, 1), ahead(i, u, 2)
                if n and norm:
                    variances(*n)
                equalities(i, u)
                if n and norm:
                    shifts(*n)
                if m:
                    masks(*m)
                scatter_rows(i, u)
                n = ahead(i, u, 4)
                if n:
                    sources(*n)

            sweep(dve, step)

        @block.scalar
        def _(act):
            def normalise(i, u):
                g = UNROLL * i + u
                act.wait_ge(ln.shift_ready, g + 1)
                for t in range(GT):
                    tile = xg[:, u, t * D:(t + 1) * D]
                    ins = ln.scaled(nc, tile, tile, t, u % 2, ACT.Relu)
                ins.then_inc(normed, 1)

            def turned_rows(i, u):
                g = UNROLL * i + u
                act.wait_ge(turned, g + 1)
                wait(act, mask_ready, NREL * (g - 1))
                nc.scalar.copy(hT[:, u % 2, :], ps[:, u % 2, :]).then_inc(hT_ready, 1)

            def messages(i, u):
                g = UNROLL * i + u
                act.wait_ge(product, g + 1)
                wait(act, pair_product, g - 1)
                nc.scalar.copy(msg[:, u % 2, :], ps[:, 2 + u % 2, :]).then_inc(msg_ready, 1)

            def sums(i, u):
                g = UNROLL * i + u
                act.wait_ge(pair_product, g + 1)
                wait(act, added, 64 * (g - 1))
                nc.scalar.copy(summed[:, u % 2, :], ps[:, 4 + u % 2, :]).then_inc(summed_ready, 1)

            def step(i, u):
                if first(i, u):
                    for k in range(2 if norm else 0):
                        ln.deviations(nc, act, c["eps"], k, k)
                        normalise(0, k)
                    turned_rows(0, 0)
                l, m, n = ahead(i, u, -2), ahead(i, u, 1), ahead(i, u, 2)
                if m:
                    turned_rows(*m)
                if l:
                    sums(*l)
                if n and norm:
                    ln.deviations(nc, act, c["eps"], n[1] % 2, UNROLL * n[0] + n[1])
                    normalise(*n)
                messages(i, u)

            sweep(act, step)
            for g in (GROUPS_E - 2, GROUPS_E - 1):
                sums(g // UNROLL, g % UNROLL)

        @block.tensor
        def _(pe):
            def turn(i, u):
                g = UNROLL * i + u
                if norm:
                    pe.wait_ge(normed, g + 1)
                else:
                    pe.wait_ge(gathered[u], 64 * (i + 1))
                wait(pe, hT_ready, g - 1)
                for t in range(GT):
                    ins = nc.tensor.transpose(ps[:, u % 2, t * P:(t + 1) * P], xg[:, u, t * D:(t + 1) * D],
                                              c["ident"][:])
                ins.then_inc(turned, 1)

            def multiply(i, u):
                g = UNROLL * i + u
                wait(pe, msg_ready, g - 1)
                for r in range(NREL):
                    pe.wait_ge(mask_ready, NREL * g + r + 1)
                    for t in range(GT):
                        ins = nc.tensor.matmul(ps[:, 2 + u % 2, t * D:(t + 1) * D],
                                               masked[:, u % 2, r, t * P:(t + 1) * P], w[:, r, :],
                                               start=(r == 0 and t == 0), stop=(r == NREL - 1),
                                               skip_group_check=True)
                ins.then_inc(product, 1)

            def add_pairs(i, u):
                g = UNROLL * i + u
                pe.wait_ge(msg_ready, g + 1)
                pe.wait_ge(same_ready, g + 1)
                wait(pe, summed_ready, g - 1)
                for t in range(GT):
                    for s in range(2):
                        other = t // 2 * 2 + s
                        ins = nc.tensor.matmul(ps[:, 4 + u % 2, t * D:(t + 1) * D],
                                               same[:, u % 2, other, (t % 2) * P:(t % 2 + 1) * P],
                                               msg[:, u % 2, other * D:(other + 1) * D],
                                               start=(s == 0), stop=(s == 1))
                ins.then_inc(pair_product, 1)

            def step(i, u):
                if first(i, u):
                    turn(0, 0)
                m, n = ahead(i, u, -1), ahead(i, u, 1)
                if n:
                    turn(*n)
                multiply(i, u)
                if m:
                    add_pairs(*m)

            sweep(pe, step)
            add_pairs(GROUPS_E // UNROLL, 0)



def edge_pass_messages(nc, sb, sem, c, ps, a):
    S = lambda n: sem(f"E3_{n}")
    ends = sb("E3_ends", [P, UNROLL, 2 * GE])
    edge = sb("E3_edge", [P, UNROLL, GT * DE])
    src_ring = sb("E3_src_ring", [P, UNROLL, GT], I32)
    dst_ring = sb("E3_dst_ring", [P, UNROLL, GT], I32)
    scat_ring = sb("E3_scat_ring", [P, UNROLL, GT], I32)
    dst_row = sb("E3_dst_row", [P, UNROLL, GE], I32)
    endsT = sb("E3_endsT", [P, 2, GE])
    edgeT = sb("E3_edgeT", [DE, GE])
    hidden = sb("E3_hidden", [P, GE])
    msg = sb("E3_msg", [P, GE])
    scaled = sb("E3_scaled", [P, GE])
    normal = sb("E3_normal", [P, 2, GE])
    same = sb("E3_same", [P, 2, GT, 2 * P])
    summedT = sb("E3_summedT", [P, GE])
    summed = sb("E3_summed", [P, 2, GE])
    lx = Stats(sb, sem, "E3x", 2 * GT)
    lm = Stats(sb, sem, "E3m", GT)
    gathered = [S(f"gathered{k}") for k in range(UNROLL)]
    rows_in = [S(f"rows_in{k}") for k in range(UNROLL)]
    ends_ready, scat_ready, added, issuing = S("ends_ready"), S("scat_ready"), S("added"), S("issuing")
    normed, turned, turned_out, hidden_product = S("normed"), S("turned"), S("turned_out"), S("hidden_product")
    hidden_ready, msg_product, msg_ready = S("hidden_ready"), S("msg_product"), S("msg_ready")
    scaled_step, normal_ready, same_ready = S("scaled_step"), S("normal_ready"), S("same_ready")
    pair_product, summedT_ready, out_product, summed_ready = (
        S("pair_product"), S("summedT_ready"), S("out_product"), S("summed_ready"))

    with nc.Block() as block:
        @block.sync
        def _(sp):
            def load(i, u):
                g = UNROLL * i + u
                wait(sp, turned, g - 3)
                wait(sp, same_ready, g - 3)
                edges = bass.ds(g * GE, GE)
                sp.dma_start(edge[:, u, :].rearrange("p (t f) -> p t f", t=GT),
                             a["edge"][edges, :].rearrange("(t p) f -> p t f", p=P)).then_inc(rows_in[u], 16)
                sp.dma_start(dst_row[:, u, :], a["dst_line"][edges].partition_broadcast(P)).then_inc(rows_in[u], 16)

            def step(i, u):
                if first(i, u):
                    for k in range(3):
                        load(0, k)
                n = ahead(i, u, 3)
                if n:
                    load(*n)

            sweep(sp, step)

        @block.gpsimd
        def _(pool):
            def gather(i, u, q):
                g = UNROLL * i + u
                if q == 0:
                    pool.wait_ge(ends_ready, 2 * g + 2)
                    wait(pool, turned, g - 3)
                    pool.sem_inc(issuing, 1)
                for t in (2 * q, 2 * q + 1):
                    for side, ring in enumerate((src_ring, dst_ring)):
                        at = (side * GT + t) * D
                        pool.indirect_dma_start(
                            ends[:, u, at:at + D], None, a["x2"],
                            bass.IndirectOffsetOnAxis(ap=ring[:, u, t:t + 1], axis=0)).then_inc(gathered[u], 16)

            def scatter(i, u, q):
                g = UNROLL * i + u
                if q == 0:
                    pool.wait_ge(summed_ready, g + 1)
                    pool.wait_ge(scat_ready, g + 1)
                wait(pool, added, 32 * (2 * g + q))
                pool.sem_inc(issuing, 1)
                for t in (2 * q, 2 * q + 1):
                    pool.indirect_dma_start(
                        a["s3"], bass.IndirectOffsetOnAxis(ap=scat_ring[:, u, t:t + 1], axis=0),
                        summed[:, u % 2, t * D:(t + 1) * D], None, compute_op=ALU.add).then_inc(added, 16)

            def step(i, u):
                if first(i, u):
                    for k in range(3):
                        gather(0, k, 0)
                        gather(0, k, 1)
                n, m = ahead(i, u, 3), ahead(i, u, -1)
                for q in range(2):
                    if n:
                        gather(*n, q)
                    if m:
                        scatter(*m, q)

            sweep(pool, step)
            scatter(GROUPS_E // UNROLL, 0, 0)
            scatter(GROUPS_E // UNROLL, 0, 1)
            pool.wait_ge(added, 64 * GROUPS_E)

        @block.vector
        def _(dve):
            def ring_rows(i, u):
                here = bass.ds((UNROLL * i + u) * GT, GT)
                wait(dve, gathered[u], 128 * i)
                nc.vector.tensor_scalar(src_ring[:, u, :], c["src"][:, here], 0.0, None, ALU.add).then_inc(ends_ready, 1)
                nc.vector.tensor_scalar(dst_ring[:, u, :], c["dst"][:, here], float(NODES - 1), None,
                                        ALU.min).then_inc(ends_ready, 1)

            def variances(i, u):
                dve.wait_ge(gathered[u], 128 * (i + 1))
                lx.variances(nc, dve, [ends[:, u, t * D:(t + 1) * D] for t in range(2 * GT)], u % 2, UNROLL * i + u)

            def normalise(i, u):
                lx.reciprocals(nc, dve, u % 2, UNROLL * i + u)
                for t in range(2 * GT):
                    tile = ends[:, u, t * D:(t + 1) * D]
                    ins = lx.normalise(nc, tile, tile, t, u % 2)
                ins.then_inc(normed, 1)

            def equalities(i, u):
                g = UNROLL * i + u
                dve.wait_ge(rows_in[u], 32 * (i + 1))
                wait(dve, pair_product, g - 1)
                for t in range(GT):
                    pair = slice(t // 2 * 2 * P, (t // 2 + 1) * 2 * P)
                    ins = nc.vector.tensor_scalar(same[:, u % 2, t, :], dst_row[:, u, pair],
                                                  c["dstf"][:, bass.ds(g * GT + t, 1)], None, ALU.is_equal)
                ins.then_inc(same_ready, 1)
                wait(dve, added, 64 * (g - 3))
                nc.vector.tensor_scalar(scat_ring[:, u, :], c["scat"][:, bass.ds(g * GT, GT)], 0.0, None, ALU.add).then_inc(scat_ready, 1)

            def message_variances(i, u):
                g = UNROLL * i + u
                dve.wait_ge(msg_ready, g + 1)
                lm.variances(nc, dve, [msg[:, t * D:(t + 1) * D] for t in range(GT)], u % 2, g)

            def message_norm(i, u):
                g = UNROLL * i + u
                lm.reciprocals(nc, dve, u % 2, g)
                for t in range(GT):
                    tile = slice(t * D, (t + 1) * D)
                    ins = lm.normalise(nc, scaled[:, tile], msg[:, tile], t, u % 2)
                ins.then_inc(scaled_step, 1)
                tiles = lambda t: t.rearrange("p (t d) -> p t d", t=GT)
                dve.wait_ge(scaled_step, 2 * g + 1)
                nc.vector.tensor_tensor(tiles(scaled[:]), tiles(scaled[:]),
                                        c["eg"][:].unsqueeze(1).broadcast_to([P, GT, D]),
                                        ALU.mult).then_inc(scaled_step, 1)
                dve.wait_ge(scaled_step, 2 * g + 2)
                wait(dve, pair_product, g - 1)
                nc.vector.tensor_tensor(tiles(normal[:, u % 2, :]), tiles(scaled[:]),
                                        c["ebeta"][:].unsqueeze(1).broadcast_to([P, GT, D]),
                                        ALU.add).then_inc(normal_ready, 1)

            def step(i, u):
                if first(i, u):
                    for k in range(UNROLL):
                        ring_rows(0, k)
                    variances(0, 0)
                    normalise(0, 0)
                n = ahead(i, u, 1)
                if n:
                    variances(*n)
                equalities(i, u)
                if n:
                    normalise(*n)
                message_variances(i, u)
                message_norm(i, u)
                n = ahead(i, u, 4)
                if n:
                    ring_rows(*n)

            sweep(dve, step)

        @block.scalar
        def _(act):
            def turned_rows(i, u):
                g = UNROLL * i + u
                act.wait_ge(turned, g + 1)
                wait(act, hidden_product, g)
                for side in range(2):
                    nc.scalar.activation(endsT[:, side, :], ps[:, side, :], ACT.Relu)
                nc.scalar.copy(edgeT[:], ps[0:DE, 2, :]).then_inc(turned_out, 1)

            def hidden_rows(i, u):
                g = UNROLL * i + u
                act.wait_ge(hidden_product, g + 1)
                wait(act, msg_product, g)
                nc.scalar.activation(hidden[:], ps[:, 3, :], ACT.Relu, bias=c["eb1"][:]).then_inc(hidden_ready, 1)

            def messages(i, u):
                g = UNROLL * i + u
                act.wait_ge(msg_product, g + 1)
                wait(act, scaled_step, 2 * g)
                nc.scalar.activation(msg[:], ps[:, 4, :], ACT.Relu).then_inc(msg_ready, 1)

            def sums_turned(i, u):
                g = UNROLL * i + u
                act.wait_ge(pair_product, g + 1)
                wait(act, out_product, g)
                nc.scalar.copy(summedT[:], ps[:, 5, :]).then_inc(summedT_ready, 1)

            def sums(i, u):
                g = UNROLL * i + u
                act.wait_ge(out_product, g + 1)
                wait(act, added, 64 * (g - 1))
                nc.scalar.copy(summed[:, u % 2, :], ps[:, 6, :]).then_inc(summed_ready, 1)

            def step(i, u):
                if first(i, u):
                    lx.deviations(nc, act, c["eps"], 0, 0)
                    turned_rows(0, 0)
                m, n = ahead(i, u, -1), ahead(i, u, 1)
                hidden_rows(i, u)
                if m:
                    sums_turned(*m)
                if n:
                    lx.deviations(nc, act, c["eps"], n[1] % 2, UNROLL * n[0] + n[1])
                messages(i, u)
                if m:
                    sums(*m)
                lm.deviations(nc, act, c["eps"], u % 2, UNROLL * i + u)
                if n:
                    turned_rows(*n)

            sweep(act, step)
            sums_turned(GROUPS_E // UNROLL, 0)
            sums(GROUPS_E // UNROLL, 0)

        @block.tensor
        def _(pe):
            def turn(i, u):
                g = UNROLL * i + u
                pe.wait_ge(normed, g + 1)
                pe.wait_ge(rows_in[u], 32 * (i + 1))
                wait(pe, turned_out, g)
                for t in range(2 * GT):
                    nc.tensor.transpose(ps[:, t // GT, (t % GT) * P:(t % GT + 1) * P],
                                        ends[:, u, t * D:(t + 1) * D], c["ident"][:])
                for t in range(GT):
                    ins = nc.tensor.transpose(ps[0:DE, 2, t * P:(t + 1) * P], edge[:, u, t * DE:(t + 1) * DE],
                                              c["ident"][:])
                ins.then_inc(turned, 1)

            def hidden_layer(i, u):
                g = UNROLL * i + u
                pe.wait_ge(turned_out, g + 1)
                wait(pe, hidden_ready, g)
                nc.tensor.matmul(ps[:, 3, :], c["eW1s"][:], endsT[:, 0, :], start=True, stop=False)
                nc.tensor.matmul(ps[:, 3, :], c["eW1d"][:], endsT[:, 1, :], start=False, stop=False)
                nc.tensor.matmul(ps[:, 3, :], c["eW1e"][:], edgeT[:], start=False, stop=True).then_inc(hidden_product, 1)

            def message_layer(i, u):
                g = UNROLL * i + u
                pe.wait_ge(hidden_ready, g + 1)
                wait(pe, msg_ready, g)
                nc.tensor.matmul(ps[:, 4, :], c["ones_row"][:], c["eb2"][:].rearrange("o k d -> o (k d)"),
                                 start=True, stop=False, skip_group_check=True)
                for t in range(GT):
                    ins = nc.tensor.matmul(ps[:, 4, t * D:(t + 1) * D], hidden[:, t * P:(t + 1) * P], c["eW2"][:],
                                           start=False, stop=True, skip_group_check=True)
                ins.then_inc(msg_product, 1)

            def add_pairs(i, u):
                g = UNROLL * i + u
                pe.wait_ge(normal_ready, g + 1)
                pe.wait_ge(same_ready, g + 1)
                wait(pe, summedT_ready, g)
                for q in range(2):
                    for s in range(2):
                        t = 2 * q + s
                        ins = nc.tensor.matmul(ps[:, 5, q * 2 * P:(q + 1) * 2 * P],
                                               normal[:, u % 2, t * D:(t + 1) * D], same[:, u % 2, t, :],
                                               start=(s == 0), stop=(s == 1))
                ins.then_inc(pair_product, 1)

            def out_layer(i, u):
                g = UNROLL * i + u
                pe.wait_ge(summedT_ready, g + 1)
                wait(pe, summed_ready, g)
                for t in range(GT):
                    ins = nc.tensor.matmul(ps[:, 6, t * D:(t + 1) * D], summedT[:, t * P:(t + 1) * P], c["nW1m"][:],
                                           start=True, stop=True)
                ins.then_inc(out_product, 1)

            def step(i, u):
                if first(i, u):
                    turn(0, 0)
                m, n = ahead(i, u, -1), ahead(i, u, 1)
                hidden_layer(i, u)
                if m:
                    add_pairs(*m)
                message_layer(i, u)
                if m:
                    out_layer(*m)
                if n:
                    turn(*n)

            sweep(pe, step)
            add_pairs(GROUPS_E // UNROLL, 0)
            out_layer(GROUPS_E // UNROLL, 0)


def graph_layers(nc, ctx, a):
    sb = lambda name, shape, dt=F32: ctx.enter_context(nc.sbuf_tensor(name, shape, dt))
    sem = lambda name: ctx.enter_context(nc.semaphore(name))
    ps = ctx.enter_context(nc.psum_tensor("ps", [P, 8, 512], F32))
    for name in ("s1", "s2", "s3"):
        a[name] = nc.dram_tensor(name, [ROWS_S, D], F32).ap()
    for name in ("y1", "x2"):
        a[name] = nc.dram_tensor(name, [NODES, D], F32).ap()
    c = setup(nc, sb, sem, a)

    def stage(build, *args):
        with ExitStack() as own:
            own_sb = lambda name, shape, dt=F32: own.enter_context(nc.sbuf_tensor(name, shape, dt))
            build(nc, own_sb, sem, c, ps, a, *args)

    stage(edge_pass_relational, "E1", a["x"], a["s1"], c["w1"], True)
    stage(node_pass_1)
    stage(edge_pass_relational, "E2", a["y1"], a["s2"], c["w2"], False)
    stage(node_pass_2)
    stage(edge_pass_messages)
    stage(node_pass_3)


_WEIGHTS = {
    "w1": "L0_gnn_w1", "sl1": "L0_gnn_sl1", "b1": "L0_gnn_b1", "w2": "L0_gnn_w2", "sl2": "L0_gnn_sl2",
    "b2": "L0_gnn_b2", "eW1": "L1_gnn_eW1", "eb1": "L1_gnn_eb1", "eW2": "L1_gnn_eW2", "eb2": "L1_gnn_eb2",
    "nW1": "L1_gnn_nW1", "nb1": "L1_gnn_nb1", "nW2": "L1_gnn_nW2", "nb2": "L1_gnn_nb2", "eg": "L1_gnn_eg",
    "ebeta": "L1_gnn_ebeta", "ng": "L1_gnn_ng", "nbeta": "L1_gnn_nbeta",
}


def kernel(**inputs):
    import numpy as np
    import concourse.bacc as bacc
    from concourse.bass_utils import run_bass_kernel_spmd

    def padded(a, fill):
        rest = np.full((TILES_E * P - EDGES,) + a.shape[1:], fill, a.dtype)
        return np.concatenate([a, rest])

    src = padded(np.asarray(inputs["src"]), 0)
    dst = padded(np.asarray(inputs["dst"]), PAD_DST)
    laid = {
        "x": np.asarray(inputs["x"]),
        "src": np.ascontiguousarray(src.reshape(TILES_E, P).T),
        "dst": np.ascontiguousarray(dst.reshape(TILES_E, P).T),
        "dst_line": dst,
        "type": padded(np.asarray(inputs["edge_type_8"]), 0),
        "edge": padded(np.asarray(inputs["edge_attr_64"]), 0),
    }
    for name, given in _WEIGHTS.items():
        laid[name] = np.ascontiguousarray(inputs[given])

    nc = bacc.Bacc("TRN2", target_bir_lowering=False, num_devices=1)
    arrays, a = {}, {}
    for name, array in laid.items():
        arrays["in_" + name] = array
        a[name] = nc.dram_tensor("in_" + name, array.shape, mybir.dt.from_np(array.dtype), kind="ExternalInput").ap()
    a["out"] = nc.dram_tensor("out_x", [NODES, D], F32, kind="ExternalOutput").ap()
    with ExitStack() as ctx:
        graph_layers(nc, ctx, a)
    r = run_bass_kernel_spmd(nc, [arrays], core_ids=[0])
    return r.results[0]["out_x"]
```

```python
from contextlib import ExitStack

import concourse.bass as bass
from concourse import mybir

F32 = mybir.dt.float32
I32 = mybir.dt.int32
BF16 = mybir.dt.bfloat16
ALU = mybir.AluOpType
ACT = mybir.ActivationFunctionType

P = 128
D = 128
DE = 64
NREL = 8
EPS = 1e-5

NODES = 50000
EDGES = 25000
TILES_E = 196
GT = 4
GROUPS_E = TILES_E // GT
GE = GT * P
DUMP = NODES
PAD_DST = DUMP + 2 * P
ROWS_S = 50432
NT = 8
GN = NT * P
GROUPS_N = 49
LAST_BASE = NODES - GN

QUARTER = P // 4

UNROLL = 4
assert GROUPS_E == GROUPS_N == 49
KEPT = 20
LOOP_END = 11


def sweep(eng, step):
    for u in range(UNROLL):
        step(0, u)
    with eng.Fori(1, LOOP_END) as i:
        for u in range(UNROLL):
            step(i, u)
    for g in range(LOOP_END * UNROLL, GROUPS_N):
        step(g // UNROLL, g % UNROLL)


def sweep_with_kept(eng, step):
    for u in range(UNROLL):
        step(0, u, None)
    with eng.Fori(1, KEPT // UNROLL - 1) as i:
        for u in range(UNROLL):
            step(i, u, "kept")
    for u in range(UNROLL):
        step(KEPT // UNROLL - 1, u, None)
    with eng.Fori(KEPT // UNROLL, LOOP_END) as i:
        for u in range(UNROLL):
            step(i, u, "rest")
    for g in range(LOOP_END * UNROLL, GROUPS_N):
        step(g // UNROLL, g % UNROLL, None)


def is_kept(i, u, reach):
    return reach == "kept" if reach else UNROLL * i + u < KEPT


def ahead(i, u, n):
    v = u + n
    j, w = i + v // UNROLL, v % UNROLL
    if isinstance(j, int) and not 0 <= UNROLL * j + w < GROUPS_N:
        return None
    return j, w


def first(i, u):
    return isinstance(i, int) and i == 0 and u == 0


def wait(eng, sem, value):
    if not (isinstance(value, int) and value <= 0):
        eng.wait_ge(sem, value)


def node_base(i, u):
    g = UNROLL * i + u
    if isinstance(g, int):
        return min(g * GN, LAST_BASE)
    return g * GN


def rows(t, base):
    return t[bass.ds(base, GN), :].rearrange("(p k) d -> p (k d)", p=P)


class Stats:

    def __init__(self, sb, sem, name, n, kept=None, shifts=True):
        self.n = n
        self.kept = kept
        self.st = sb(name + "_ln_st", [P, n, 6])
        self.small = sb(name + "_ln_small", [P, 4, n])
        self.mean, self.var, self.sd, self.rstd, self.shift = kept or [
            sb(name + "_ln_" + t, [P, UNROLL, n]) for t in ("mean", "var", "sd", "rstd", "shift")]
        self.step = sem(name + "_ln_step")
        self.var_ready = sem(name + "_ln_var_ready")
        self.sd_ready = sem(name + "_ln_sd_ready")
        self.rstd_ready = sem(name + "_ln_rstd_ready")
        self.shift_ready = sem(name + "_ln_shift_ready") if shifts else None

    def group(self, t, slot):
        return t[:, bass.ds(slot * self.n, self.n)] if self.kept else t[:, slot, :]

    def tile(self, t, slot, k):
        return t[:, bass.ds(slot * self.n + k, 1)] if self.kept else t[:, slot, k:k + 1]

    def variances(self, nc, dve, tiles, slot, g):
        self.halves(nc, tiles)
        self.sums(nc, dve, g)
        self.means(nc, dve, slot, g)
        self.totals(nc, dve, slot, g)

    def halves(self, nc, tiles):
        for k in range(self.n):
            ins = nc.vector.bn_stats(self.st[:, k, :], tiles[k])
        ins.then_inc(self.step, 1)

    def sums(self, nc, dve, g):
        st, small = self.st, self.small
        dve.wait_ge(self.step, 3 * g + 1)
        nc.vector.tensor_tensor(small[:, 0, :], st[:, :, 1], st[:, :, 4], ALU.subtract)
        nc.vector.tensor_tensor(small[:, 1, :], st[:, :, 1], st[:, :, 4], ALU.add)
        nc.vector.tensor_tensor(small[:, 2, :], st[:, :, 2], st[:, :, 5], ALU.add).then_inc(self.step, 1)

    def means(self, nc, dve, slot, g):
        small = self.small
        dve.wait_ge(self.step, 3 * g + 2)
        nc.vector.tensor_scalar(self.group(self.mean, slot), small[:, 1, :], 0.5, None, ALU.mult)
        nc.vector.scalar_tensor_tensor(out=small[:, 3, :], in0=small[:, 0, :], scalar=D / 4.0,
                                       in1=small[:, 0, :], op0=ALU.mult, op1=ALU.mult).then_inc(self.step, 1)

    def totals(self, nc, dve, slot, g):
        dve.wait_ge(self.step, 3 * g + 3)
        nc.vector.tensor_tensor(self.group(self.var, slot), self.small[:, 3, :], self.small[:, 2, :],
                                ALU.add).then_inc(self.var_ready, 1)

    def deviations(self, nc, act, eps, slot, g):
        act.wait_ge(self.var_ready, g + 1)
        nc.scalar.activation(self.group(self.sd, slot), self.group(self.var, slot), ACT.Sqrt, bias=eps[:],
                             scale=1.0 / D).then_inc(self.sd_ready, 1)

    def reciprocals(self, nc, dve, slot, g):
        dve.wait_ge(self.sd_ready, g + 1)
        nc.vector.reciprocal(self.group(self.rstd, slot), self.group(self.sd, slot)).then_inc(self.rstd_ready, 1)
        dve.wait_ge(self.rstd_ready, g + 1)

    def shifts(self, nc, slot):
        nc.vector.scalar_tensor_tensor(out=self.group(self.shift, slot), in0=self.group(self.mean, slot),
                                       scalar=-1.0, in1=self.group(self.rstd, slot), op0=ALU.mult,
                                       op1=ALU.mult).then_inc(self.shift_ready, 1)

    def scaled(self, nc, out, in_, k, slot, func):
        return nc.scalar.activation(out, in_, func, bias=self.tile(self.shift, slot, k),
                                    scale=self.tile(self.rstd, slot, k))

    def normalise(self, engine, out, in_, k, slot):
        return engine.tensor_scalar(out, in_, self.tile(self.mean, slot, k), self.tile(self.rstd, slot, k),
                                    ALU.subtract, ALU.mult)


def setup(nc, sb, sem, a):
    c = {}

    def keep(name, shape, dt=F32):
        c[name] = sb("c_" + name, shape, dt)
        return c[name]

    ident = keep("ident", [P, P])
    earlier = keep("earlier", [P, 2, 2 * P])
    eps = keep("eps", [P, 1])
    one = keep("one", [P, 1])
    zeros = keep("zeros", [P, 4 * D])
    ones_row = keep("ones_row", [1, P])
    nb2_parts = keep("nb2_parts", [3 * QUARTER, 4, D], BF16)
    parts_weight = keep("parts_weight", [3 * QUARTER, P], BF16)
    part = sb("c_part", [P, D], BF16)
    rest = sb("c_rest", [P, D])
    src = keep("src", [P, TILES_E], I32)
    dst = keep("dst", [P, TILES_E], I32)
    dstf = keep("dstf", [P, TILES_E])
    dump_less_dst = keep("dump_less_dst", [P, TILES_E])
    keep("scat", [P, TILES_E], I32)
    dump = keep("dump", [P, TILES_E])
    for name in ("x2_mean", "x2_var", "x2_sd", "x2_rstd", "x2_shift"):
        keep(name, [P, GROUPS_N * NT])

    first_loads = [(src[:], a["src"]), (dst[:], a["dst"])]
    for out, in_ in ((keep("sl1", [P, D])[:], a["sl1"]),
                     (keep("nb2", [P, D])[:], a["nb2"].partition_broadcast(P))):
        first_loads.append((out, in_))
    loads = []
    for name in ("w1", "w2"):
        loads.append((keep(name, [P, NREL, D])[:], a[name].rearrange("r d f -> d r f")))
    for name in ("sl2", "eW2", "nW2"):
        loads.append((keep(name, [P, D])[:], a[name]))
    loads.append((keep("eW1s", [P, D])[:], a["eW1"][0:D, :]))
    loads.append((keep("eW1d", [P, D])[:], a["eW1"][D:2 * D, :]))
    loads.append((keep("eW1e", [DE, D])[:], a["eW1"][2 * D:2 * D + DE, :]))
    loads.append((keep("nW1x", [P, D])[:], a["nW1"][0:D, :]))
    loads.append((keep("nW1m", [P, D])[:], a["nW1"][D:2 * D, :]))
    for name in ("b2", "eg", "ebeta", "ng", "nbeta"):
        loads.append((keep(name, [P, D])[:], a[name].partition_broadcast(P)))
    for name in ("b1", "eb1", "nb1"):
        loads.append((keep(name, [P, 1])[:], a[name].unsqueeze(1)))
    t = keep("eb2", [1, 4, D])
    for k in range(4):
        loads.append((t[0:1, k, :], a["eb2"].unsqueeze(0)))

    loaded, pool_done, dve_done = sem("loaded"), sem("pool_done"), sem("dve_done")
    c["weights_loaded"], c["weights_all"] = sem("weights_loaded"), 16 * len(loads)
    c["issuing"] = sem("issuing")
    with nc.Block() as block:
        @block.sync
        def _(sp):
            for out, in_ in first_loads:
                sp.dma_start(out, in_).then_inc(loaded, 16)
            sp.wait_ge(dve_done, 1)
            for s in ("s1", "s2", "s3"):
                sp.dma_start(a[s][NODES:ROWS_S, :].rearrange("(p k) d -> p (k d)", k=4),
                             zeros[0:(ROWS_S - NODES) // 4, :]).then_inc(loaded, 16)
            for out, in_ in loads:
                sp.dma_start(out, in_).then_inc(c["weights_loaded"], 16)
            sp.wait_ge(loaded, 16 * (len(first_loads) + 3))

        @block.vector
        def _(dve):
            nc.vector.memset(zeros[:], 0.0).then_inc(dve_done, 1)
            nc.vector.memset(eps[:], EPS)
            nc.vector.memset(one[:], 1.0)
            nc.vector.memset(ones_row[:], 1.0)
            dve.wait_ge(loaded, 16 * (len(first_loads) + 3))
            nc.vector.tensor_copy(dstf[:], dst[:]).then_inc(dve_done, 1)
            dve.wait_ge(dve_done, 2)
            dve.wait_ge(pool_done, 5)
            nc.vector.tensor_tensor(dump_less_dst[:], dump[:], dstf[:], ALU.subtract)
            nc.vector.memset(parts_weight[:], 1.0 / QUARTER)
            left = c["nb2"]
            for k in range(3):
                nc.vector.tensor_copy(part[:], left[:]).then_inc(dve_done, 1)
                dve.wait_ge(dve_done, 3 * k + 3)
                quarter = slice(k * QUARTER, (k + 1) * QUARTER)
                for j in range(4):
                    ins = nc.vector.tensor_copy(nb2_parts[quarter, j, :], part[quarter, :])
                ins.then_inc(dve_done, 1)
                nc.vector.tensor_tensor(rest[:], left[:], part[:], ALU.subtract).then_inc(dve_done, 1)
                dve.wait_ge(dve_done, 3 * k + 5)
                left = rest

        @block.gpsimd
        def _(pool):
            nc.gpsimd.memset(ident[:], 0.0).then_inc(pool_done, 1)
            nc.gpsimd.memset(earlier[:], 1.0).then_inc(pool_done, 1)
            pool.wait_ge(pool_done, 2)
            nc.gpsimd.affine_select(out=ident[:], in_=ident[:], compare_op=ALU.not_equal, fill=1.0, base=0,
                                    pattern=[[-1, P]], channel_multiplier=1).then_inc(pool_done, 1)
            nc.gpsimd.affine_select(out=earlier[:], in_=earlier[:], compare_op=ALU.is_gt, fill=0.0, base=0,
                                    pattern=[[P, 2], [-1, 2 * P]], channel_multiplier=1).then_inc(pool_done, 1)
            nc.gpsimd.iota(dump[:], pattern=[[0, TILES_E // 2], [P, 2]], base=DUMP, channel_multiplier=1,
                           allow_small_or_imprecise_dtypes=True).then_inc(pool_done, 1)
            pool.wait_ge(pool_done, 5)
    return c


def last_store(sp, stored, g):
    if isinstance(g, int) and g == GROUPS_N - 1:
        sp.wait_ge(stored[1 - g % 2], 16 * (g // 2))


def all_stored(sp, stored):
    sp.wait_ge(stored[0], 16 * (GROUPS_N // 2 + 1))
    sp.wait_ge(stored[1], 16 * (GROUPS_N // 2))


def tiles_of(t):
    return t.rearrange("p (k d) -> p k d", d=D)


def each_tile(row, n):
    return row[:].unsqueeze(1).broadcast_to([P, n, D])


class EdgeRows:
    AHEAD = 3

    def __init__(self, sb, sem, c, name):
        self.c = c
        self.xg = sb(f"{name}_xg", [P, UNROLL, GE])
        self.gathered = [sem(f"{name}_gathered{k}") for k in range(UNROLL)]

    def first_gathers(self, pool, x):
        for u in range(self.AHEAD):
            for t in range(GT):
                k = u * GT + t
                pool.indirect_dma_start(
                    self.xg[:, u, t * D:(t + 1) * D], None, x,
                    bass.IndirectOffsetOnAxis(ap=self.c["src"][:, k:k + 1], axis=0)).then_inc(self.gathered[u], 16)


def node_product(nc, sb, sem, c, ps, a, name, x, s, w, norm, edges):
    S = lambda n: sem(f"{name}_{n}")
    ON_ACT, ON_POOL = 3, 2
    ON_DVE = NT - ON_ACT - ON_POOL
    xin = sb(f"{name}_xin", [P, UNROLL, NT * D])
    hT = sb(f"{name}_hT", [P, 2, NT * D])
    out = sb(f"{name}_out", [P, 2, NT * D])
    ln = Stats(sb, sem, name, NT) if norm else None
    loaded = [S(f"loaded{k}") for k in range(UNROLL)]
    stored = [S(f"stored{k}") for k in range(2)]
    if norm:
        normed, act_normed, pool_normed = S("normed"), S("act_normed"), S("pool_normed")
    turned, hT_ready, product, out_ready = S("turned"), S("hT_ready"), S("product"), S("out_ready")

    def results(eng, copy, i, u):
        g = UNROLL * i + u
        wait(eng, stored[u % 2], 16 * (2 * i + u // 2))
        for h in range(2):
            eng.wait_ge(product, 2 * g + h + 1)
            copy(out[:, u % 2, h * 512:(h + 1) * 512], ps[:, 4 + 2 * (u % 2) + h, :]).then_inc(out_ready, 1)

    with nc.Block() as block:
        @block.sync
        def _(sp):
            def load(i, u):
                g = UNROLL * i + u
                wait(sp, turned, 2 * (g - 3))
                sp.dma_start(xin[:, u, :], rows(x, node_base(i, u))).then_inc(loaded[u], 16)

            def store(i, u):
                g = UNROLL * i + u
                last_store(sp, stored, g)
                sp.wait_ge(out_ready, 2 * g + 2)
                sp.dma_start(rows(s, node_base(i, u)), out[:, u % 2, :]).then_inc(stored[u % 2], 16)

            def step(i, u):
                if first(i, u):
                    for k in range(UNROLL):
                        sp.dma_start(xin[:, k, :], rows(x, node_base(0, k))).then_inc(loaded[k], 16)
                m, n = ahead(i, u, -1), ahead(i, u, 4)
                if n:
                    load(*n)
                if m:
                    store(*m)

            sweep(sp, step)
            store(GROUPS_N // UNROLL, 0)
            all_stored(sp, stored)
            if norm:
                sp.wait_ge(c["weights_loaded"], c["weights_all"])

        @block.gpsimd
        def _(pool):
            def step(i, u):
                pool.wait_ge(ln.rstd_ready, UNROLL * i + u + 1)
                pool.sem_inc(c["issuing"], 1)
                for k in range(ON_DVE, ON_DVE + ON_POOL):
                    tile = xin[:, u, k * D:(k + 1) * D]
                    ins = ln.normalise(nc.gpsimd, tile, tile, k, u)
                ins.then_inc(pool_normed, 1)

            edges.first_gathers(pool, x)
            if norm:
                sweep(pool, step)

        @block.vector
        def _(dve):
            def rows_here(i, u):
                g = UNROLL * i + u
                dve.wait_ge(loaded[u], 16 * (i + 1))
                wait(dve, act_normed, g - 3)
                wait(dve, pool_normed, g - 3)
                ln.halves(nc, [xin[:, u, k * D:(k + 1) * D] for k in range(NT)])

            def statistics(i, u):
                g = UNROLL * i + u
                ln.sums(nc, dve, g)
                ln.means(nc, dve, u, g)
                ln.totals(nc, dve, u, g)

            def both(n, m):
                g = UNROLL * n[0] + n[1]
                rows_here(*n)
                ln.reciprocals(nc, dve, m[1], UNROLL * m[0] + m[1])
                ln.sums(nc, dve, g)
                ln.shifts(nc, m[1])
                normalise(*m, range(0, 1))
                ln.means(nc, dve, n[1], g)
                normalise(*m, range(1, 2))
                ln.totals(nc, dve, n[1], g)
                normalise(*m, range(2, ON_DVE)).then_inc(normed, 1)

            def normalise(i, u, tiles):
                for k in tiles:
                    tile = xin[:, u, k * D:(k + 1) * D]
                    ins = ln.normalise(nc.vector, tile, tile, k, u)
                return ins

            def step(i, u):
                if not norm:
                    results(dve, nc.vector.tensor_copy, i, u)
                    return
                if first(i, u):
                    rows_here(0, 0)
                    statistics(0, 0)
                    both((0, 1), (0, 0))
                    both((0, 2), (0, 1))
                n, m = ahead(i, u, 3), ahead(i, u, 2)
                if n:
                    both(n, m)
                elif m:
                    ln.reciprocals(nc, dve, m[1], UNROLL * m[0] + m[1])
                    ln.shifts(nc, m[1])
                    normalise(*m, range(ON_DVE)).then_inc(normed, 1)

            sweep(dve, step)

        @block.scalar
        def _(act):
            def normalise(i, u):
                g = UNROLL * i + u
                act.wait_ge(ln.shift_ready, g + 1)
                for k in range(NT - ON_ACT, NT):
                    tile = xin[:, u, k * D:(k + 1) * D]
                    ins = ln.scaled(nc, tile, tile, k, u, ACT.Identity)
                ins.then_inc(act_normed, 1)

            def turned_rows(i, u):
                g = UNROLL * i + u
                wait(act, product, 2 * (g - 1))
                for h in range(2):
                    act.wait_ge(turned, 2 * g + h + 1)
                    half, bank = hT[:, u % 2, h * 512:(h + 1) * 512], ps[:, 2 * (u % 2) + h, :]
                    if norm:
                        ins = nc.scalar.activation(half, bank, ACT.Relu)
                    else:
                        ins = nc.scalar.activation(half, bank, ACT.Relu, bias=c["b1"][:])
                    ins.then_inc(hT_ready, 1)

            def step(i, u):
                if first(i, u):
                    if norm:
                        ln.deviations(nc, act, c["eps"], 0, 0)
                        for k in range(2):
                            ln.deviations(nc, act, c["eps"], k + 1, k + 1)
                            normalise(0, k)
                    turned_rows(0, 0)
                m, n, l = ahead(i, u, 1), ahead(i, u, 2), ahead(i, u, 3)
                if m:
                    turned_rows(*m)
                if n and norm:
                    normalise(*n)
                if l and norm:
                    ln.deviations(nc, act, c["eps"], l[1], UNROLL * l[0] + l[1])
                if norm:
                    results(act, nc.scalar.copy, i, u)

            sweep(act, step)

        @block.tensor
        def _(pe):
            def turn(i, u):
                g = UNROLL * i + u
                if norm:
                    pe.wait_ge(normed, g + 1)
                    pe.wait_ge(pool_normed, g + 1)
                    pe.wait_ge(act_normed, g + 1)
                else:
                    pe.wait_ge(loaded[u], 16 * (i + 1))
                wait(pe, hT_ready, 2 * (g - 1))
                for k in range(NT):
                    ins = nc.tensor.transpose(ps[:, 2 * (u % 2) + k // 4, (k % 4) * P:(k % 4 + 1) * P],
                                              xin[:, u, k * D:(k + 1) * D], c["ident"][:])
                    if k % 4 == 3:
                        ins.then_inc(turned, 1)

            def multiply(i, u):
                g = UNROLL * i + u
                wait(pe, out_ready, 2 * (g - 1))
                for h in range(2):
                    pe.wait_ge(hT_ready, 2 * g + h + 1)
                    for k in range(4):
                        at = h * 512 + k * P
                        ins = nc.tensor.matmul(ps[:, 4 + 2 * (u % 2) + h, k * D:(k + 1) * D],
                                               hT[:, u % 2, at:at + P], w[:], start=True, stop=True)
                    ins.then_inc(product, 1)

            def step(i, u):
                if first(i, u):
                    turn(0, 0)
                n = ahead(i, u, 1)
                if n:
                    turn(*n)
                multiply(i, u)

            sweep(pe, step)


def node_pass_2(nc, sb, sem, c, ps, a, kept):
    S = lambda n: sem(f"N2_{n}")
    ON_ACT = 5
    sin = sb("N2_sin", [P, UNROLL, NT * D])
    xin = sb("N2_xin", [P, UNROLL, NT * D])
    x2 = sb("N2_x2", [P, UNROLL, NT * D])
    h = sb("N2_h", [P, 2, NT * D])
    hT = sb("N2_hT", [P, 2, NT * D])
    out = sb("N2_out", [P, 2, NT * D])
    ln = Stats(sb, sem, "N2", NT, [c["x2_" + t] for t in ("mean", "var", "sd", "rstd", "shift")])
    loaded = [S(f"loaded{k}") for k in range(UNROLL)]
    x2_stored = [S(f"x2_stored{k}") for k in range(UNROLL)]
    stored = [S(f"stored{k}") for k in range(2)]
    biased, x2_ready, normed, act_normed, turned = (
        S("biased"), S("x2_ready"), S("normed"), S("act_normed"), S("turned"))
    hT_ready, product, out_ready = S("hT_ready"), S("product"), S("out_ready")

    def landed(i, u, reach):
        return 16 * (i + 1) if is_kept(i, u, reach) else 32 * (i + 1) - 16 * (KEPT // UNROLL)

    with nc.Block() as block:
        @block.sync
        def _(sp):
            def load(i, u, reach):
                wait(sp, x2_ready, UNROLL * i + u - 3)
                sp.dma_start(sin[:, u, :], rows(a["s2"], node_base(i, u))).then_inc(loaded[u], 16)
                if not is_kept(i, u, reach):
                    sp.dma_start(xin[:, u, :], rows(a["x"], node_base(i, u))).then_inc(loaded[u], 16)

            def store_x2(i, u):
                g = UNROLL * i + u
                if isinstance(g, int) and g == GROUPS_N - 1:
                    sp.wait_ge(x2_stored[(g - 1) % UNROLL], 16 * (g // UNROLL))
                sp.wait_ge(x2_ready, g + 1)
                sp.dma_start(rows(a["x2"], node_base(i, u)), x2[:, u, :]).then_inc(x2_stored[u], 16)

            def store(i, u):
                g = UNROLL * i + u
                last_store(sp, stored, g)
                sp.wait_ge(out_ready, 2 * g + 2)
                sp.dma_start(rows(a["s3"], node_base(i, u)), out[:, u % 2, :]).then_inc(stored[u % 2], 16)

            def step(i, u, reach):
                if first(i, u):
                    for k in range(UNROLL):
                        load(0, k, None)
                m, n = ahead(i, u, -2), ahead(i, u, 4)
                store_x2(i, u)
                if n:
                    load(*n, reach)
                if m:
                    store(*m)

            sweep_with_kept(sp, step)
            for g in (GROUPS_N - 2, GROUPS_N - 1):
                store(g // UNROLL, g % UNROLL)
            all_stored(sp, stored)
            for k in range(UNROLL):
                sp.wait_ge(x2_stored[k], 16 * ((GROUPS_N - 1 - k) // UNROLL + 1))

        @block.gpsimd
        def _(pool):
            def step(i, u, reach):
                pool.wait_ge(loaded[u], landed(i, u, reach))
                nc.gpsimd.tensor_tensor(tiles_of(sin[:, u, :]), tiles_of(sin[:, u, :]), each_tile(c["b2"], NT),
                                        ALU.add).then_inc(biased, 1)

            sweep_with_kept(pool, step)

        @block.vector
        def _(dve):
            def updated(i, u, reach):
                g = UNROLL * i + u
                if is_kept(i, u, reach):
                    x = kept[:, bass.ds(g * NT * D, NT * D)]
                else:
                    x = xin[:, u, :]
                    dve.wait_ge(loaded[u], landed(i, u, reach))
                dve.wait_ge(biased, g + 1)
                wait(dve, act_normed, g - 3)
                wait(dve, x2_stored[u], 16 * i)
                nc.vector.scalar_tensor_tensor(out=x2[:, u, :], in0=sin[:, u, :], scalar=0.0, in1=x,
                                               op0=ALU.max, op1=ALU.add).then_inc(x2_ready, 1)

            def halves(i, u):
                dve.wait_ge(x2_ready, UNROLL * i + u + 1)
                ln.halves(nc, [x2[:, u, k * D:(k + 1) * D] for k in range(NT)])

            def reciprocals(i, u):
                g = UNROLL * i + u
                ln.reciprocals(nc, dve, g, g)

            def normalise(i, u, tiles):
                g = UNROLL * i + u
                if tiles[0] == 0:
                    wait(dve, turned, 2 * (g - 1))
                for k in tiles:
                    cols = slice(k * D, (k + 1) * D)
                    ins = ln.normalise(nc.vector, h[:, u % 2, cols], x2[:, u, cols], k, g)
                return ins

            def both(n, m, reach):
                g = UNROLL * n[0] + n[1]
                updated(*n, reach)
                reciprocals(*m)
                halves(*n)
                ln.shifts(nc, UNROLL * m[0] + m[1])
                ln.sums(nc, dve, g)
                normalise(*m, range(1))
                ln.means(nc, dve, g, g)
                normalise(*m, range(1, 2))
                ln.totals(nc, dve, g, g)
                normalise(*m, range(2, NT - ON_ACT)).then_inc(normed, 1)

            def step(i, u, reach):
                if first(i, u):
                    updated(0, 0, None)
                    halves(0, 0)
                    ln.sums(nc, dve, 0)
                    ln.means(nc, dve, 0, 0)
                    ln.totals(nc, dve, 0, 0)
                    both((0, 1), (0, 0), None)
                    both((0, 2), (0, 1), None)
                n, m = ahead(i, u, 3), ahead(i, u, 2)
                if n:
                    both(n, m, reach)
                elif m:
                    reciprocals(*m)
                    ln.shifts(nc, UNROLL * m[0] + m[1])
                    normalise(*m, range(NT - ON_ACT)).then_inc(normed, 1)

            sweep_with_kept(dve, step)

        @block.scalar
        def _(act):
            def normalise(i, u):
                g = UNROLL * i + u
                act.wait_ge(ln.shift_ready, g + 1)
                wait(act, turned, 2 * (g - 1))
                for k in range(NT - ON_ACT, NT):
                    cols = slice(k * D, (k + 1) * D)
                    ins = ln.scaled(nc, h[:, u % 2, cols], x2[:, u, cols], k, g, ACT.Identity)
                ins.then_inc(act_normed, 1)

            def turned_rows(i, u):
                g = UNROLL * i + u
                wait(act, product, 2 * (g - 1))
                for k in range(2):
                    act.wait_ge(turned, 2 * g + k + 1)
                    nc.scalar.activation(hT[:, u % 2, k * 512:(k + 1) * 512], ps[:, 2 * (u % 2) + k, :],
                                         ACT.Relu).then_inc(hT_ready, 1)

            def results(i, u):
                g = UNROLL * i + u
                wait(act, stored[u % 2], 16 * (2 * i + u // 2))
                for k in range(2):
                    act.wait_ge(product, 2 * g + k + 1)
                    nc.scalar.copy(out[:, u % 2, k * 512:(k + 1) * 512],
                                   ps[:, 4 + 2 * (u % 2) + k, :]).then_inc(out_ready, 1)

            def step(i, u):
                if first(i, u):
                    ln.deviations(nc, act, c["eps"], 0, 0)
                    for k in range(2):
                        ln.deviations(nc, act, c["eps"], k + 1, k + 1)
                        normalise(0, k)
                    turned_rows(0, 0)
                m, n, l = ahead(i, u, 1), ahead(i, u, 2), ahead(i, u, 3)
                if m:
                    turned_rows(*m)
                if n:
                    normalise(*n)
                if l:
                    g = UNROLL * l[0] + l[1]
                    ln.deviations(nc, act, c["eps"], g, g)
                results(i, u)

            sweep(act, step)

        @block.tensor
        def _(pe):
            def turn(i, u):
                g = UNROLL * i + u
                pe.wait_ge(normed, g + 1)
                pe.wait_ge(act_normed, g + 1)
                wait(pe, hT_ready, 2 * (g - 1))
                for k in range(NT):
                    ins = nc.tensor.transpose(ps[:, 2 * (u % 2) + k // 4, (k % 4) * P:(k % 4 + 1) * P],
                                              h[:, u % 2, k * D:(k + 1) * D], c["ident"][:])
                    if k % 4 == 3:
                        ins.then_inc(turned, 1)

            def multiply(i, u):
                g = UNROLL * i + u
                wait(pe, out_ready, 2 * (g - 1))
                for half in range(2):
                    pe.wait_ge(hT_ready, 2 * g + half + 1)
                    for k in range(4):
                        at = half * 512 + k * P
                        ins = nc.tensor.matmul(ps[:, 4 + 2 * (u % 2) + half, k * D:(k + 1) * D],
                                               hT[:, u % 2, at:at + P], c["nW1x"][:], start=True, stop=True)
                    ins.then_inc(product, 1)

            def step(i, u):
                if first(i, u):
                    turn(0, 0)
                n = ahead(i, u, 1)
                if n:
                    turn(*n)
                multiply(i, u)

            sweep(pe, step)


def node_pass_3(nc, sb, sem, c, ps, a):
    S = lambda n: sem(f"N3_{n}")
    ON_ACT = 3
    xin = sb("N3_xin", [P, UNROLL, NT * D])
    sin = sb("N3_sin", [P, UNROLL, NT * D])
    base = sb("N3_base", [P, UNROLL, NT * D])
    h = sb("N3_h", [P, UNROLL, NT * D])
    hidT = sb("N3_hidT", [P, 2, NT * D])
    res = sb("N3_res", [P, UNROLL, NT * D])
    ln = Stats(sb, sem, "N3", NT)
    loaded = [S(f"loaded{k}") for k in range(UNROLL)]
    stored = [S(f"stored{k}") for k in range(UNROLL)]
    h_ready, turned, hidT_ready, product = S("h_ready"), S("turned"), S("hidT_ready"), S("product")
    base_ready, normed, act_normed, scaled, out_ready = (
        S("base_ready"), S("normed"), S("act_normed"), S("scaled"), S("out_ready"))

    def v(u, k):
        return ps[:, 4 + 2 * (u % 2) + k // 4, (k % 4) * D:(k % 4 + 1) * D]

    with nc.Block() as block:
        @block.sync
        def _(sp):
            def load(i, u):
                g = UNROLL * i + u
                wait(sp, turned, 2 * (g - 3))
                wait(sp, h_ready, 2 * (g - 3))
                wait(sp, base_ready, g - 3)
                sp.dma_start(xin[:, u, :], rows(a["x2"], node_base(i, u))).then_inc(loaded[u], 16)
                sp.dma_start(sin[:, u, :], rows(a["s3"], node_base(i, u))).then_inc(loaded[u], 16)

            def store(i, u):
                g = UNROLL * i + u
                if isinstance(g, int) and g == GROUPS_N - 1:
                    sp.wait_ge(stored[(g - 1) % UNROLL], 16 * (g // UNROLL))
                sp.wait_ge(out_ready, 2 * g + 2)
                sp.dma_start(rows(a["out"], node_base(i, u)), res[:, u, :]).then_inc(stored[u], 16)

            def step(i, u):
                if first(i, u):
                    for k in range(UNROLL):
                        load(0, k)
                m, n = ahead(i, u, -4), ahead(i, u, 4)
                if n:
                    load(*n)
                if m:
                    store(*m)

            sweep(sp, step)
            for g in range(GROUPS_N - 4, GROUPS_N):
                store(g // UNROLL, g % UNROLL)
            for k in range(UNROLL):
                sp.wait_ge(stored[k], 16 * ((GROUPS_N - 1 - k) // UNROLL + 1))

        @block.scalar
        def _(act):
            LOWER, UPPER = range(0, NT // 2), range(NT // 2, NT)

            def rows_h(i, u, tiles):
                g = UNROLL * i + u
                act.wait_ge(loaded[u], 32 * (i + 1))
                wait(act, product, 2 * (g - 3))
                for k in tiles:
                    cols = slice(k * D, (k + 1) * D)
                    at = bass.ds(g * NT + k, 1)
                    ins = nc.scalar.activation(h[:, u, cols], xin[:, u, cols], ACT.Relu,
                                               bias=c["x2_shift"][:, at], scale=c["x2_rstd"][:, at])
                ins.then_inc(h_ready, 1)

            def hidden_rows(i, u):
                g = UNROLL * i + u
                wait(act, product, 2 * (g - 1))
                for half in range(2):
                    act.wait_ge(turned, 2 * g + half + 1)
                    nc.scalar.activation(hidT[:, u % 2, half * 512:(half + 1) * 512],
                                         ps[:, 2 * (u % 2) + half, :], ACT.Relu,
                                         bias=c["nb1"][:]).then_inc(hidT_ready, 1)

            def outer_norm(i, u):
                g = UNROLL * i + u
                act.wait_ge(ln.shift_ready, g + 1)
                wait(act, stored[u], 16 * i)
                for k in range(NT - ON_ACT, NT):
                    cols = slice(k * D, (k + 1) * D)
                    ins = ln.scaled(nc, res[:, u, cols], v(u, k), k, u, ACT.Identity)
                ins.then_inc(act_normed, 1)

            def step(i, u):
                if first(i, u):
                    rows_h(0, 0, LOWER)
                    rows_h(0, 0, UPPER)
                    hidden_rows(0, 0)
                    rows_h(0, 1, LOWER)
                    rows_h(0, 1, UPPER)
                m, n, l = ahead(i, u, -1), ahead(i, u, 1), ahead(i, u, 2)
                if n:
                    hidden_rows(*n)
                if l:
                    rows_h(*l, LOWER)
                if m:
                    ln.deviations(nc, act, c["eps"], m[1], UNROLL * m[0] + m[1])
                if l:
                    rows_h(*l, UPPER)
                if m:
                    outer_norm(*m)

            sweep(act, step)
            ln.deviations(nc, act, c["eps"], 0, GROUPS_N - 1)
            outer_norm(GROUPS_N // UNROLL, 0)

        @block.tensor
        def _(pe):
            def turn(i, u):
                g = UNROLL * i + u
                pe.wait_ge(loaded[u], 32 * (i + 1))
                wait(pe, hidT_ready, 2 * (g - 1))
                for k in range(NT):
                    ins = nc.tensor.transpose(ps[:, 2 * (u % 2) + k // 4, (k % 4) * P:(k % 4 + 1) * P],
                                              sin[:, u, k * D:(k + 1) * D], c["ident"][:])
                    if k % 4 == 3:
                        ins.then_inc(turned, 1)

            def multiply(i, u):
                g = UNROLL * i + u
                pe.wait_ge(h_ready, 2 * g + 2)
                wait(pe, normed, g - 1)
                wait(pe, act_normed, g - 1)
                for half in range(2):
                    bank = ps[:, 4 + 2 * (u % 2) + half, :]
                    nc.tensor.matmul(bank, c["parts_weight"][:], c["nb2_parts"][:].rearrange("p k d -> p (k d)"),
                                     start=True, stop=False, skip_group_check=True)
                    nc.tensor.matmul(bank, c["ident"][:], h[:, u, half * 512:(half + 1) * 512],
                                     start=False, stop=False, skip_group_check=True)
                    pe.wait_ge(hidT_ready, 2 * g + half + 1)
                    for k in range(4):
                        at = half * 512 + k * P
                        ins = nc.tensor.matmul(bank[:, k * D:(k + 1) * D], hidT[:, u % 2, at:at + P],
                                               c["nW2"][:], start=False, stop=True, skip_group_check=True)
                    ins.then_inc(product, 1)

            def step(i, u):
                if first(i, u):
                    turn(0, 0)
                n = ahead(i, u, 1)
                if n:
                    turn(*n)
                multiply(i, u)

            sweep(pe, step)

        @block.gpsimd
        def _(pool):
            def bases(i, u):
                g = UNROLL * i + u
                pool.wait_ge(loaded[u], 32 * (i + 1))
                wait(pool, out_ready, 2 * (g - 3))
                nc.gpsimd.tensor_tensor(tiles_of(base[:, u, :]), tiles_of(xin[:, u, :]), each_tile(c["nbeta"], NT),
                                        ALU.add).then_inc(base_ready, 1)

            def scale(i, u):
                g = UNROLL * i + u
                pool.wait_ge(normed, g + 1)
                pool.wait_ge(act_normed, g + 1)
                nc.gpsimd.tensor_tensor(tiles_of(res[:, u, :]), tiles_of(res[:, u, :]), each_tile(c["ng"], NT),
                                        ALU.mult).then_inc(scaled, 1)

            def step(i, u):
                m = ahead(i, u, -2)
                bases(i, u)
                if m:
                    scale(*m)

            sweep(pool, step)
            for g in range(GROUPS_N - 2, GROUPS_N):
                scale(g // UNROLL, g % UNROLL)

        @block.vector
        def _(dve):
            def halves(i, u):
                g = UNROLL * i + u
                dve.wait_ge(product, 2 * g + 2)
                wait(dve, act_normed, g - 3)
                ln.halves(nc, [v(u, k) for k in range(NT)])

            def statistics(i, u):
                g = UNROLL * i + u
                ln.sums(nc, dve, g)
                ln.means(nc, dve, u, g)
                ln.totals(nc, dve, u, g)

            def normalise(i, u):
                g = UNROLL * i + u
                ln.reciprocals(nc, dve, u, g)
                wait(dve, stored[u], 16 * i)
                for k in reversed(range(NT - ON_ACT)):
                    cols = slice(k * D, (k + 1) * D)
                    ins = ln.normalise(nc.vector, res[:, u, cols], v(u, k), k, u)
                    if k == NT // 2:
                        ln.shifts(nc, u)
                ins.then_inc(normed, 1)

            def finish(i, u, half):
                dve.wait_ge(scaled, UNROLL * i + u + 1)
                cols = slice(half * 512, (half + 1) * 512)
                nc.vector.tensor_tensor(res[:, u, cols], res[:, u, cols], base[:, u, cols],
                                        ALU.add).then_inc(out_ready, 1)

            def step(i, u):
                l, m = ahead(i, u, -3), ahead(i, u, -1)
                if m:
                    halves(*m)
                if l:
                    finish(*l, 0)
                if m:
                    statistics(*m)
                if l:
                    finish(*l, 1)
                if m:
                    normalise(*m)

            sweep(dve, step)
            halves(GROUPS_N // UNROLL, 0)
            statistics(GROUPS_N // UNROLL, 0)
            normalise(GROUPS_N // UNROLL, 0)
            for g in range(GROUPS_N - 3, GROUPS_N):
                finish(g // UNROLL, g % UNROLL, 0)
                finish(g // UNROLL, g % UNROLL, 1)


def edge_pass_relational(nc, sb, sem, c, ps, a, name, x, s, w, norm, edges, kept=None):
    S = lambda n: sem(f"{name}_{n}")
    xg, gathered = edges.xg, edges.gathered
    src_ring = sb(f"{name}_src_ring", [P, UNROLL, GT], I32)
    scat_ring = sb(f"{name}_scat_ring", [P, UNROLL, GT], I32)
    type_row = sb(f"{name}_type_row", [P, UNROLL, GE], I32)
    dst_row = sb(f"{name}_dst_row", [P, UNROLL, GE], I32)
    hT = sb(f"{name}_hT", [P, 2, GE])
    masked = sb(f"{name}_masked", [P, 2, NREL, GE])
    PARTS = 1 if norm else 3
    msg = sb(f"{name}_msg", [P, 2, PARTS, GE], F32 if norm else BF16)
    same = sb(f"{name}_same", [P, 2, GT, 2 * P], F32 if norm else BF16)
    summed = sb(f"{name}_summed", [P, 2, GE])
    ln = Stats(sb, sem, name, GT) if norm else None
    if norm:
        before = sb(f"{name}_before", [P, GT, 2 * P])
        count = sb(f"{name}_count", [P, GT])
        shift = sb(f"{name}_move", [P, GT])
        scat_step = S("scat_step")
    rows_in = [S(f"rows_in{k}") for k in range(UNROLL)]
    src_ready, scat_ready, added = S("src_ready"), S("scat_ready"), S("added")
    normed = S("normed") if norm else None
    turned, hT_ready, mask_ready = S("turned"), S("hT_ready"), S("mask_ready")
    product, msg_step, same_step = S("product"), S("msg_step"), S("same_step")
    pair_product, summed_ready = S("pair_product"), S("summed_ready")

    x_kept = S("x_kept") if kept is not None else None
    MSG_STEPS = 1
    if not norm:
        rest = sb(f"{name}_rest", [P, GE])
        MSG_STEPS = 4

    with nc.Block() as block:
        @block.sync
        def _(sp):
            def load(i, u):
                g = UNROLL * i + u
                wait(sp, same_step, 2 * (g - 3))
                wait(sp, scat_ready, g - 3)
                edges = bass.ds(g * GE, GE)
                sp.dma_start(type_row[:, u, :], a["type"][edges].partition_broadcast(P)).then_inc(rows_in[u], 16)
                sp.dma_start(dst_row[:, u, :], a["dst_line"][edges].partition_broadcast(P)).then_inc(rows_in[u], 16)

            def step(i, u):
                if first(i, u):
                    for k in range(3):
                        load(0, k)
                n = ahead(i, u, 3)
                if n:
                    load(*n)
                if kept is not None and not isinstance(i, int) and u % 2 == 0:
                    k = 2 * i - 2 + u // 2
                    sp.dma_start(kept[:, bass.ds(k * NT * D, NT * D)], rows(a["x"], k * GN)).then_inc(x_kept, 16)

            sweep(sp, step)
            if kept is not None:
                sp.wait_ge(x_kept, 16 * KEPT)

        @block.gpsimd
        def _(pool):
            def gather(i, u, q):
                g = UNROLL * i + u
                if q == 0:
                    pool.wait_ge(src_ready, g - edges.AHEAD + 1)
                    wait(pool, turned, g - 3)
                    pool.sem_inc(c["issuing"], 1)
                for t in (2 * q, 2 * q + 1):
                    pool.indirect_dma_start(
                        xg[:, u, t * D:(t + 1) * D], None, x,
                        bass.IndirectOffsetOnAxis(ap=src_ring[:, u, t:t + 1], axis=0)).then_inc(gathered[u], 16)

            def scatter(i, u, q):
                g = UNROLL * i + u
                if q == 0:
                    pool.wait_ge(summed_ready, g + 1)
                    pool.wait_ge(scat_ready, g + 1)
                wait(pool, added, 32 * (2 * g + q))
                pool.sem_inc(c["issuing"], 1)
                for t in (2 * q, 2 * q + 1):
                    pool.indirect_dma_start(
                        s, bass.IndirectOffsetOnAxis(ap=scat_ring[:, u, t:t + 1], axis=0),
                        summed[:, u % 2, t * D:(t + 1) * D], None, compute_op=ALU.add).then_inc(added, 16)

            def step(i, u):
                n, m = ahead(i, u, edges.AHEAD), ahead(i, u, -2)
                for q in range(2):
                    if n:
                        gather(*n, q)
                    if m:
                        scatter(*m, q)

            sweep(pool, step)
            for g in (GROUPS_E - 2, GROUPS_E - 1):
                scatter(g // UNROLL, g % UNROLL, 0)
                scatter(g // UNROLL, g % UNROLL, 1)
            pool.wait_ge(added, 64 * GROUPS_E)

        @block.vector
        def _(dve):
            def sources(i, u):
                g = UNROLL * i + u
                wait(dve, gathered[u], 64 * i)
                nc.vector.tensor_scalar(src_ring[:, u, :], c["src"][:, bass.ds(g * GT, GT)], 0.0, None, ALU.add).then_inc(src_ready, 1)

            def rows_here(i, u):
                dve.wait_ge(gathered[u], 64 * (i + 1))
                wait(dve, normed, UNROLL * i + u - 3)
                ln.halves(nc, [xg[:, u, t * D:(t + 1) * D] for t in range(GT)])

            def shifts(i, u):
                ln.reciprocals(nc, dve, u, UNROLL * i + u)
                ln.shifts(nc, u)

            def masks(i, u, relations):
                g = UNROLL * i + u
                if relations[0] == 0:
                    dve.wait_ge(rows_in[u], 32 * (i + 1))
                    dve.wait_ge(hT_ready, g + 1)
                    wait(dve, product, g - 1)
                for r in relations:
                    nc.vector.scalar_tensor_tensor(out=masked[:, u % 2, r, :], in0=type_row[:, u, :],
                                                   scalar=float(r), in1=hT[:, u % 2, :],
                                                   op0=ALU.is_equal, op1=ALU.mult).then_inc(mask_ready, 1)

            def count_earlier(i, u, t):
                g = UNROLL * i + u
                if t == 0:
                    dve.wait_ge(rows_in[u], 32 * (i + 1))
                    wait(dve, scat_step, 3 * g)
                pair = slice(t // 2 * 2 * P, (t // 2 + 1) * 2 * P)
                ins = nc.vector.scalar_tensor_tensor(
                    out=before[:, t, :], in0=dst_row[:, u, pair], scalar=c["dstf"][:, bass.ds(g * GT + t, 1)],
                    in1=c["earlier"][:, t % 2, :], op0=ALU.is_equal, op1=ALU.mult, accum_out=count[:, t:t + 1])
                if t == GT - 1:
                    ins.then_inc(scat_step, 1)

            def ways_to_dump(i, u):
                g = UNROLL * i + u
                dve.wait_ge(scat_step, 3 * g + 1)
                nc.vector.scalar_tensor_tensor(out=shift[:], in0=count[:], scalar=1.0,
                                               in1=c["dump_less_dst"][:, bass.ds(g * GT, GT)],
                                               op0=ALU.min, op1=ALU.mult).then_inc(scat_step, 1)

            def scatter_rows(i, u):
                g = UNROLL * i + u
                here = bass.ds(g * GT, GT)
                dve.wait_ge(scat_step, 3 * g + 2)
                nc.vector.tensor_tensor(c["scat"][:, here], shift[:], c["dstf"][:, here],
                                        ALU.add).then_inc(scat_step, 1)

            def message_parts(i, u):
                g = UNROLL * i + u
                bank, parts = ps[:, 2 + u % 2, :], msg[:, u % 2, :, :]
                dve.wait_ge(product, g + 1)
                wait(dve, pair_product, g - 1)
                nc.vector.tensor_scalar(parts[:, 0, :], bank, 0.0, None, ALU.add).then_inc(msg_step, 1)
                dve.wait_ge(msg_step, 4 * g + 1)
                nc.vector.tensor_tensor(rest[:], bank, parts[:, 0, :], ALU.subtract).then_inc(msg_step, 1)
                dve.wait_ge(msg_step, 4 * g + 2)
                nc.vector.tensor_scalar(parts[:, 1, :], rest[:], 0.0, None, ALU.add).then_inc(msg_step, 1)
                dve.wait_ge(msg_step, 4 * g + 3)
                nc.vector.tensor_tensor(parts[:, 2, :], rest[:], parts[:, 1, :], ALU.subtract).then_inc(msg_step, 1)

            def scatter_ring(i, u):
                g = UNROLL * i + u
                if norm:
                    dve.wait_ge(scat_step, 3 * g + 3)
                wait(dve, added, 64 * (g - 3))
                nc.vector.tensor_scalar(scat_ring[:, u, :], c["scat"][:, bass.ds(g * GT, GT)], 0.0, None,
                                        ALU.add).then_inc(scat_ready, 1)

            def step(i, u):
                if first(i, u):
                    for k in range(edges.AHEAD, UNROLL):
                        sources(0, k)
                    for k in range(2 if norm else 0):
                        rows_here(0, k)
                        ln.sums(nc, dve, k)
                        ln.means(nc, dve, k, k)
                        ln.totals(nc, dve, k, k)
                        shifts(0, k)
                    masks(0, 0, range(NREL))
                m, n = ahead(i, u, 1), ahead(i, u, 2)
                if norm:
                    if n:
                        g = UNROLL * n[0] + n[1]
                        rows_here(*n)
                    count_earlier(i, u, 0)
                    if n:
                        ln.sums(nc, dve, g)
                    count_earlier(i, u, 1)
                    if n:
                        ln.means(nc, dve, n[1], g)
                    count_earlier(i, u, 2)
                    if n:
                        ln.totals(nc, dve, n[1], g)
                    count_earlier(i, u, 3)
                    ways_to_dump(i, u)
                    if n:
                        shifts(*n)
                    scatter_rows(i, u)
                l = ahead(i, u, -1)
                if l and not norm:
                    message_parts(*l)
                if m:
                    masks(*m, range(1))
                scatter_ring(i, u)
                if m:
                    masks(*m, range(1, NREL))
                n = ahead(i, u, 4)
                if n:
                    sources(*n)

            sweep(dve, step)
            if not norm:
                message_parts(GROUPS_E // UNROLL, 0)

        @block.scalar
        def _(act):
            def normalise(i, u):
                g = UNROLL * i + u
                act.wait_ge(ln.shift_ready, g + 1)
                for t in range(GT):
                    tile = xg[:, u, t * D:(t + 1) * D]
                    ins = ln.scaled(nc, tile, tile, t, u, ACT.Relu)
                ins.then_inc(normed, 1)

            def turned_rows(i, u):
                g = UNROLL * i + u
                act.wait_ge(turned, g + 1)
                wait(act, mask_ready, NREL * (g - 1))
                if norm:
                    ins = nc.scalar.copy(hT[:, u % 2, :], ps[:, u % 2, :])
                else:
                    ins = nc.scalar.activation(hT[:, u % 2, :], ps[:, u % 2, :], ACT.Relu, bias=c["b1"][:])
                ins.then_inc(hT_ready, 1)

            def equalities(i, u):
                g = UNROLL * i + u
                act.wait_ge(rows_in[u], 32 * (i + 1))
                wait(act, pair_product, g - 1)
                for t in range(GT):
                    pair = slice(t // 2 * 2 * P, (t // 2 + 1) * 2 * P)
                    ins = nc.scalar.activation(same[:, u % 2, t, :], dst_row[:, u, pair], ACT.Square,
                                               bias=c["dstf"][:, bass.ds(g * GT + t, 1)], scale=-1.0)
                ins.then_inc(same_step, 1)
                act.wait_ge(same_step, 2 * g + 1)
                nc.scalar.activation(same[:, u % 2, :, :], same[:, u % 2, :, :], ACT.Relu, bias=c["one"][:],
                                     scale=-1.0).then_inc(same_step, 1)

            def messages(i, u):
                g = UNROLL * i + u
                act.wait_ge(product, g + 1)
                wait(act, pair_product, g - 1)
                nc.scalar.copy(msg[:, u % 2, 0, :], ps[:, 2 + u % 2, :]).then_inc(msg_step, 1)

            def sums(i, u):
                g = UNROLL * i + u
                act.wait_ge(pair_product, g + 1)
                wait(act, added, 64 * (g - 1))
                nc.scalar.copy(summed[:, u % 2, :], ps[:, 4 + u % 2, :]).then_inc(summed_ready, 1)

            def step(i, u):
                if first(i, u):
                    for k in range(2 if norm else 0):
                        ln.deviations(nc, act, c["eps"], k, k)
                        normalise(0, k)
                    turned_rows(0, 0)
                l, m, n = ahead(i, u, -2), ahead(i, u, 1), ahead(i, u, 2)
                if m:
                    turned_rows(*m)
                if l:
                    sums(*l)
                equalities(i, u)
                if n and norm:
                    ln.deviations(nc, act, c["eps"], n[1], UNROLL * n[0] + n[1])
                    normalise(*n)
                if norm:
                    messages(i, u)

            sweep(act, step)
            for g in (GROUPS_E - 2, GROUPS_E - 1):
                sums(g // UNROLL, g % UNROLL)

        @block.tensor
        def _(pe):
            def turn(i, u):
                g = UNROLL * i + u
                if norm:
                    pe.wait_ge(normed, g + 1)
                else:
                    pe.wait_ge(gathered[u], 64 * (i + 1))
                wait(pe, hT_ready, g - 1)
                for t in range(GT):
                    ins = nc.tensor.transpose(ps[:, u % 2, t * P:(t + 1) * P], xg[:, u, t * D:(t + 1) * D],
                                              c["ident"][:])
                ins.then_inc(turned, 1)

            def multiply(i, u):
                g = UNROLL * i + u
                wait(pe, msg_step, MSG_STEPS * (g - 1))
                for r in range(NREL):
                    pe.wait_ge(mask_ready, NREL * g + r + 1)
                    for t in range(GT):
                        ins = nc.tensor.matmul(ps[:, 2 + u % 2, t * D:(t + 1) * D],
                                               masked[:, u % 2, r, t * P:(t + 1) * P], w[:, r, :],
                                               start=(r == 0 and t == 0), stop=(r == NREL - 1),
                                               skip_group_check=True)
                ins.then_inc(product, 1)

            def add_pairs(i, u):
                g = UNROLL * i + u
                pe.wait_ge(msg_step, MSG_STEPS * (g + 1))
                pe.wait_ge(same_step, 2 * g + 2)
                wait(pe, summed_ready, g - 1)
                for t in range(GT):
                    for s in range(2):
                        other = t // 2 * 2 + s
                        for p in range(PARTS):
                            ins = nc.tensor.matmul(ps[:, 4 + u % 2, t * D:(t + 1) * D],
                                                   same[:, u % 2, other, (t % 2) * P:(t % 2 + 1) * P],
                                                   msg[:, u % 2, p, other * D:(other + 1) * D],
                                                   start=(s == 0 and p == 0), stop=(s == 1 and p == PARTS - 1))
                ins.then_inc(pair_product, 1)

            def step(i, u):
                if first(i, u):
                    turn(0, 0)
                m, n = ahead(i, u, -1), ahead(i, u, 1)
                if n:
                    turn(*n)
                multiply(i, u)
                if m:
                    add_pairs(*m)

            sweep(pe, step)
            add_pairs(GROUPS_E // UNROLL, 0)



def edge_pass_messages(nc, sb, sem, c, ps, a):
    S = lambda n: sem(f"E3_{n}")
    ends = sb("E3_ends", [P, UNROLL, 2 * GE])
    edge = sb("E3_edge", [P, UNROLL, GT * DE])
    src_ring = sb("E3_src_ring", [P, UNROLL, GT], I32)
    dst_ring = sb("E3_dst_ring", [P, UNROLL, GT], I32)
    scat_ring = sb("E3_scat_ring", [P, UNROLL, GT], I32)
    dst_row = sb("E3_dst_row", [P, UNROLL, GE], I32)
    endsT = sb("E3_endsT", [P, 2, GE])
    edgeT = sb("E3_edgeT", [DE, GE])
    hidden = sb("E3_hidden", [P, GE])
    msg = sb("E3_msg", [P, GE])
    scaled = sb("E3_scaled", [P, GE])
    normal = sb("E3_normal", [P, 2, GE])
    same = sb("E3_same", [P, 2, GT, 2 * P])
    summedT = sb("E3_summedT", [P, GE])
    summed = sb("E3_summed", [P, 2, GE])
    lx = Stats(sb, sem, "E3x", 2 * GT, shifts=False)
    lm = Stats(sb, sem, "E3m", GT, shifts=False)
    gathered = [S(f"gathered{k}") for k in range(UNROLL)]
    rows_in = [S(f"rows_in{k}") for k in range(UNROLL)]
    ends_ready, scat_ready, added = S("ends_ready"), S("scat_ready"), S("added")
    normed, turned, turned_out, hidden_product = S("normed"), S("turned"), S("turned_out"), S("hidden_product")
    hidden_ready, msg_product, msg_ready = S("hidden_ready"), S("msg_product"), S("msg_ready")
    scaled_step, normal_ready, same_ready = S("scaled_step"), S("normal_ready"), S("same_ready")
    pair_product, summedT_ready, out_product, summed_ready = (
        S("pair_product"), S("summedT_ready"), S("out_product"), S("summed_ready"))

    with nc.Block() as block:
        @block.sync
        def _(sp):
            def load(i, u):
                g = UNROLL * i + u
                wait(sp, turned, g - 3)
                wait(sp, same_ready, g - 3)
                edges = bass.ds(g * GE, GE)
                sp.dma_start(edge[:, u, :].rearrange("p (t f) -> p t f", t=GT),
                             a["edge"][edges, :].rearrange("(t p) f -> p t f", p=P)).then_inc(rows_in[u], 16)
                sp.dma_start(dst_row[:, u, :], a["dst_line"][edges].partition_broadcast(P)).then_inc(rows_in[u], 16)

            def step(i, u):
                if first(i, u):
                    for k in range(3):
                        load(0, k)
                n = ahead(i, u, 3)
                if n:
                    load(*n)

            sweep(sp, step)

        @block.gpsimd
        def _(pool):
            def gather(i, u, q):
                g = UNROLL * i + u
                if q == 0:
                    pool.wait_ge(ends_ready, 2 * g + 2)
                    wait(pool, turned, g - 3)
                    pool.sem_inc(c["issuing"], 1)
                for t in (2 * q, 2 * q + 1):
                    for side, ring in enumerate((src_ring, dst_ring)):
                        at = (side * GT + t) * D
                        pool.indirect_dma_start(
                            ends[:, u, at:at + D], None, a["x2"],
                            bass.IndirectOffsetOnAxis(ap=ring[:, u, t:t + 1], axis=0)).then_inc(gathered[u], 16)

            def scatter(i, u, q):
                g = UNROLL * i + u
                if q == 0:
                    pool.wait_ge(summed_ready, g + 1)
                    pool.wait_ge(scat_ready, g + 1)
                wait(pool, added, 32 * (2 * g + q))
                pool.sem_inc(c["issuing"], 1)
                for t in (2 * q, 2 * q + 1):
                    pool.indirect_dma_start(
                        a["s3"], bass.IndirectOffsetOnAxis(ap=scat_ring[:, u, t:t + 1], axis=0),
                        summed[:, u % 2, t * D:(t + 1) * D], None, compute_op=ALU.add).then_inc(added, 16)

            def step(i, u):
                if first(i, u):
                    for k in range(3):
                        gather(0, k, 0)
                        gather(0, k, 1)
                n, m = ahead(i, u, 3), ahead(i, u, -1)
                for q in range(2):
                    if n:
                        gather(*n, q)
                    if m:
                        scatter(*m, q)

            sweep(pool, step)
            scatter(GROUPS_E // UNROLL, 0, 0)
            scatter(GROUPS_E // UNROLL, 0, 1)
            pool.wait_ge(added, 64 * GROUPS_E)

        @block.vector
        def _(dve):
            def ring_rows(i, u):
                here = bass.ds((UNROLL * i + u) * GT, GT)
                wait(dve, gathered[u], 128 * i)
                nc.vector.tensor_scalar(src_ring[:, u, :], c["src"][:, here], 0.0, None, ALU.add).then_inc(ends_ready, 1)
                nc.vector.tensor_scalar(dst_ring[:, u, :], c["dst"][:, here], float(NODES - 1), None,
                                        ALU.min).then_inc(ends_ready, 1)

            def variances(i, u):
                dve.wait_ge(gathered[u], 128 * (i + 1))
                lx.variances(nc, dve, [ends[:, u, t * D:(t + 1) * D] for t in range(2 * GT)], u, UNROLL * i + u)

            def normalise(i, u):
                lx.reciprocals(nc, dve, u, UNROLL * i + u)
                for t in range(2 * GT):
                    tile = ends[:, u, t * D:(t + 1) * D]
                    ins = lx.normalise(nc.vector, tile, tile, t, u)
                ins.then_inc(normed, 1)

            def equalities(i, u):
                g = UNROLL * i + u
                dve.wait_ge(rows_in[u], 32 * (i + 1))
                wait(dve, pair_product, g - 1)
                for t in range(GT):
                    pair = slice(t // 2 * 2 * P, (t // 2 + 1) * 2 * P)
                    ins = nc.vector.tensor_scalar(same[:, u % 2, t, :], dst_row[:, u, pair],
                                                  c["dstf"][:, bass.ds(g * GT + t, 1)], None, ALU.is_equal)
                ins.then_inc(same_ready, 1)
                wait(dve, added, 64 * (g - 3))
                nc.vector.tensor_scalar(scat_ring[:, u, :], c["scat"][:, bass.ds(g * GT, GT)], 0.0, None, ALU.add).then_inc(scat_ready, 1)

            def message_variances(i, u):
                g = UNROLL * i + u
                dve.wait_ge(msg_ready, g + 1)
                lm.variances(nc, dve, [msg[:, t * D:(t + 1) * D] for t in range(GT)], u, g)

            def message_norm(i, u):
                g = UNROLL * i + u
                lm.reciprocals(nc, dve, u, g)
                for t in range(GT):
                    tile = slice(t * D, (t + 1) * D)
                    ins = lm.normalise(nc.vector, scaled[:, tile], msg[:, tile], t, u)
                ins.then_inc(scaled_step, 1)
                tiles = lambda t: t.rearrange("p (t d) -> p t d", t=GT)
                dve.wait_ge(scaled_step, 2 * g + 1)
                nc.vector.tensor_tensor(tiles(scaled[:]), tiles(scaled[:]),
                                        c["eg"][:].unsqueeze(1).broadcast_to([P, GT, D]),
                                        ALU.mult).then_inc(scaled_step, 1)
                dve.wait_ge(scaled_step, 2 * g + 2)
                wait(dve, pair_product, g - 1)
                nc.vector.tensor_tensor(tiles(normal[:, u % 2, :]), tiles(scaled[:]),
                                        c["ebeta"][:].unsqueeze(1).broadcast_to([P, GT, D]),
                                        ALU.add).then_inc(normal_ready, 1)

            def step(i, u):
                if first(i, u):
                    for k in range(UNROLL):
                        ring_rows(0, k)
                    variances(0, 0)
                    normalise(0, 0)
                n = ahead(i, u, 1)
                if n:
                    variances(*n)
                equalities(i, u)
                if n:
                    normalise(*n)
                message_variances(i, u)
                message_norm(i, u)
                n = ahead(i, u, 4)
                if n:
                    ring_rows(*n)

            sweep(dve, step)

        @block.scalar
        def _(act):
            def turned_rows(i, u):
                g = UNROLL * i + u
                act.wait_ge(turned, g + 1)
                wait(act, hidden_product, g)
                for side in range(2):
                    nc.scalar.activation(endsT[:, side, :], ps[:, side, :], ACT.Relu)
                nc.scalar.copy(edgeT[:], ps[0:DE, 2, :]).then_inc(turned_out, 1)

            def hidden_rows(i, u):
                g = UNROLL * i + u
                act.wait_ge(hidden_product, g + 1)
                wait(act, msg_product, g)
                nc.scalar.activation(hidden[:], ps[:, 3, :], ACT.Relu, bias=c["eb1"][:]).then_inc(hidden_ready, 1)

            def messages(i, u):
                g = UNROLL * i + u
                act.wait_ge(msg_product, g + 1)
                wait(act, scaled_step, 2 * g)
                nc.scalar.activation(msg[:], ps[:, 4, :], ACT.Relu).then_inc(msg_ready, 1)

            def sums_turned(i, u):
                g = UNROLL * i + u
                act.wait_ge(pair_product, g + 1)
                wait(act, out_product, g)
                nc.scalar.copy(summedT[:], ps[:, 5, :]).then_inc(summedT_ready, 1)

            def sums(i, u):
                g = UNROLL * i + u
                act.wait_ge(out_product, g + 1)
                wait(act, added, 64 * (g - 1))
                nc.scalar.copy(summed[:, u % 2, :], ps[:, 6, :]).then_inc(summed_ready, 1)

            def step(i, u):
                if first(i, u):
                    lx.deviations(nc, act, c["eps"], 0, 0)
                    turned_rows(0, 0)
                m, n = ahead(i, u, -1), ahead(i, u, 1)
                hidden_rows(i, u)
                if m:
                    sums_turned(*m)
                if n:
                    lx.deviations(nc, act, c["eps"], n[1], UNROLL * n[0] + n[1])
                messages(i, u)
                if m:
                    sums(*m)
                lm.deviations(nc, act, c["eps"], u, UNROLL * i + u)
                if n:
                    turned_rows(*n)

            sweep(act, step)
            sums_turned(GROUPS_E // UNROLL, 0)
            sums(GROUPS_E // UNROLL, 0)

        @block.tensor
        def _(pe):
            def turn(i, u):
                g = UNROLL * i + u
                pe.wait_ge(normed, g + 1)
                pe.wait_ge(rows_in[u], 32 * (i + 1))
                wait(pe, turned_out, g)
                for t in range(2 * GT):
                    nc.tensor.transpose(ps[:, t // GT, (t % GT) * P:(t % GT + 1) * P],
                                        ends[:, u, t * D:(t + 1) * D], c["ident"][:])
                for t in range(GT):
                    ins = nc.tensor.transpose(ps[0:DE, 2, t * P:(t + 1) * P], edge[:, u, t * DE:(t + 1) * DE],
                                              c["ident"][:])
                ins.then_inc(turned, 1)

            def hidden_layer(i, u):
                g = UNROLL * i + u
                pe.wait_ge(turned_out, g + 1)
                wait(pe, hidden_ready, g)
                nc.tensor.matmul(ps[:, 3, :], c["eW1s"][:], endsT[:, 0, :], start=True, stop=False)
                nc.tensor.matmul(ps[:, 3, :], c["eW1d"][:], endsT[:, 1, :], start=False, stop=False)
                nc.tensor.matmul(ps[:, 3, :], c["eW1e"][:], edgeT[:], start=False, stop=True).then_inc(hidden_product, 1)

            def message_layer(i, u):
                g = UNROLL * i + u
                pe.wait_ge(hidden_ready, g + 1)
                wait(pe, msg_ready, g)
                nc.tensor.matmul(ps[:, 4, :], c["ones_row"][:], c["eb2"][:].rearrange("o k d -> o (k d)"),
                                 start=True, stop=False, skip_group_check=True)
                for t in range(GT):
                    ins = nc.tensor.matmul(ps[:, 4, t * D:(t + 1) * D], hidden[:, t * P:(t + 1) * P], c["eW2"][:],
                                           start=False, stop=True, skip_group_check=True)
                ins.then_inc(msg_product, 1)

            def add_pairs(i, u):
                g = UNROLL * i + u
                pe.wait_ge(normal_ready, g + 1)
                pe.wait_ge(same_ready, g + 1)
                wait(pe, summedT_ready, g)
                for q in range(2):
                    for s in range(2):
                        t = 2 * q + s
                        ins = nc.tensor.matmul(ps[:, 5, q * 2 * P:(q + 1) * 2 * P],
                                               normal[:, u % 2, t * D:(t + 1) * D], same[:, u % 2, t, :],
                                               start=(s == 0), stop=(s == 1))
                ins.then_inc(pair_product, 1)

            def out_layer(i, u):
                g = UNROLL * i + u
                pe.wait_ge(summedT_ready, g + 1)
                wait(pe, summed_ready, g)
                for t in range(GT):
                    ins = nc.tensor.matmul(ps[:, 6, t * D:(t + 1) * D], summedT[:, t * P:(t + 1) * P], c["nW1m"][:],
                                           start=True, stop=True)
                ins.then_inc(out_product, 1)

            def step(i, u):
                if first(i, u):
                    turn(0, 0)
                m, n = ahead(i, u, -1), ahead(i, u, 1)
                hidden_layer(i, u)
                if m:
                    add_pairs(*m)
                message_layer(i, u)
                if m:
                    out_layer(*m)
                if n:
                    turn(*n)

            sweep(pe, step)
            add_pairs(GROUPS_E // UNROLL, 0)
            out_layer(GROUPS_E // UNROLL, 0)


def graph_layers(nc, ctx, a):
    sb = lambda name, shape, dt=F32: ctx.enter_context(nc.sbuf_tensor(name, shape, dt))
    sem = lambda name: ctx.enter_context(nc.semaphore(name))
    ps = ctx.enter_context(nc.psum_tensor("ps", [P, 8, 512], F32))
    for name in ("s1", "s2", "s3"):
        a[name] = nc.dram_tensor(name, [ROWS_S, D], F32).ap()
    a["x2"] = nc.dram_tensor("x2", [NODES, D], F32).ap()
    c = setup(nc, sb, sem, a)

    def stage(build, *args):
        with ExitStack() as own:
            own_sb = lambda name, shape, dt=F32: own.enter_context(nc.sbuf_tensor(name, shape, dt))
            build(nc, own_sb, sem, c, ps, a, *args)

    for node_name, edge_name, x, s, node_weight, edge_weight, norm in (
            ("N0", "E1", a["x"], a["s1"], c["sl1"], c["w1"], True),
            ("N1", "E2", a["s1"], a["s2"], c["sl2"], c["w2"], False)):
        with ExitStack() as shared:
            shared_sb = lambda name, shape, dt=F32: shared.enter_context(nc.sbuf_tensor(name, shape, dt))
            kept = None if norm else shared_sb("x_kept", [P, KEPT * NT * D])
            with ExitStack() as both:
                both_sb = lambda name, shape, dt=F32: both.enter_context(nc.sbuf_tensor(name, shape, dt))
                edges = EdgeRows(both_sb, sem, c, edge_name)
                stage(node_product, node_name, x, s, node_weight, norm, edges)
                stage(edge_pass_relational, edge_name, x, s, edge_weight, norm, edges, kept)
            if not norm:
                stage(node_pass_2, kept)
    stage(edge_pass_messages)
    stage(node_pass_3)


_WEIGHTS = {
    "w1": "L0_gnn_w1", "sl1": "L0_gnn_sl1", "b1": "L0_gnn_b1", "w2": "L0_gnn_w2", "sl2": "L0_gnn_sl2",
    "b2": "L0_gnn_b2", "eW1": "L1_gnn_eW1", "eb1": "L1_gnn_eb1", "eW2": "L1_gnn_eW2", "eb2": "L1_gnn_eb2",
    "nW1": "L1_gnn_nW1", "nb1": "L1_gnn_nb1", "nW2": "L1_gnn_nW2", "nb2": "L1_gnn_nb2", "eg": "L1_gnn_eg",
    "ebeta": "L1_gnn_ebeta", "ng": "L1_gnn_ng", "nbeta": "L1_gnn_nbeta",
}


def kernel(**inputs):
    import numpy as np
    import concourse.bacc as bacc
    from concourse.bass_utils import run_bass_kernel_spmd

    def padded(a, fill):
        rest = np.full((TILES_E * P - EDGES,) + a.shape[1:], fill, a.dtype)
        return np.concatenate([a, rest])

    src = padded(np.asarray(inputs["src"]), 0)
    dst = padded(np.asarray(inputs["dst"]), PAD_DST)
    laid = {
        "x": np.asarray(inputs["x"]),
        "src": np.ascontiguousarray(src.reshape(TILES_E, P).T),
        "dst": np.ascontiguousarray(dst.reshape(TILES_E, P).T),
        "dst_line": dst,
        "type": padded(np.asarray(inputs["edge_type_8"]), 0),
        "edge": padded(np.asarray(inputs["edge_attr_64"]), 0),
    }
    for name, given in _WEIGHTS.items():
        laid[name] = np.ascontiguousarray(inputs[given])

    nc = bacc.Bacc("TRN2", target_bir_lowering=False, num_devices=1)
    arrays, a = {}, {}
    for name, array in laid.items():
        arrays["in_" + name] = array
        a[name] = nc.dram_tensor("in_" + name, array.shape, mybir.dt.from_np(array.dtype), kind="ExternalInput").ap()
    a["out"] = nc.dram_tensor("out_x", [NODES, D], F32, kind="ExternalOutput").ap()
    with ExitStack() as ctx:
        graph_layers(nc, ctx, a)
    r = run_bass_kernel_spmd(nc, [arrays], core_ids=[0])
    return r.results[0]["out_x"]
```
